# Optimizing a Trainium2 kernel written in Bass

```python
import numpy as np
import jax
import jax.numpy as jnp

def _softmax(x, axis=-1):
    return jax.nn.softmax(x, axis=axis)

def _gelu(x):
    return jax.nn.gelu(x, approximate=True)

def _silu(x):
    return jax.nn.silu(x)

def _sigmoid(x):
    return jax.nn.sigmoid(x)

def _layernorm(x, axis=-1, eps=1e-05):
    m = jnp.mean(x, axis=axis, keepdims=True)
    v = jnp.var(x, axis=axis, keepdims=True)
    return (x - m) / jnp.sqrt(v + eps)

def _scatter_add(tgt, idx, src, axis=0):
    return tgt.at[idx].add(src)

def _segment_sum(src, seg, n):
    return jax.ops.segment_sum(src, seg, n)
kernel_name = 'mk_cond_resid_d4_seqx_r4_45e015'

def setup_inputs(seed: int=0):
    np.random.seed(seed)
    _w = jnp.asarray

    def _rec_inputs():
        import jax
        import jax.numpy as jnp
        _rk = jax.random.key(seed)
        x = -0.000125 + 0.9999 * jax.random.normal(jax.random.fold_in(_rk, 1), (2, 1024, 256), jnp.float32)
        _lenS = 1024 - jax.random.randint(jax.random.fold_in(_rk, 7), (2,), 0, max(1, 1024 // 4) + 1, jnp.int32)
        _lenS2 = 1024 - jax.random.randint(jax.random.fold_in(_rk, 8), (2,), 0, max(1, 1024 // 4) + 1, jnp.int32)
        cond_1024 = 0.00782532 + 1.00527 * jax.random.normal(jax.random.fold_in(_rk, 11), (2, 256), jnp.float32)
        return (x, cond_1024)
    x, cond_1024 = _rec_inputs()

    def _L0_cond_setup():
        import jax, jax.numpy as jnp
        import numpy as np
        B, S, D = (8, 1024, 256)
        H = 16
        HD = D // H
        ACT_DIM = 256
        key = jax.random.key(seed)
        ks = jax.random.split(key, 10)
        s = 0.02
        return {'hidden_states': jax.random.normal(ks[0], (B, S, D), jnp.float32), 'activation': jax.random.normal(ks[1], (B, ACT_DIM), jnp.float32), 'W_q': jax.random.normal(ks[2], (D, D), jnp.float32) * s, 'b_q': jnp.zeros((D,), jnp.float32), 'W_kv': jax.random.normal(ks[3], (ACT_DIM, 2 * D), jnp.float32) * s, 'b_kv': jnp.zeros((2 * D,), jnp.float32), 'no_op_k': jax.random.normal(ks[4], (1, H, 1, HD), jnp.float32) * s, 'no_op_v': jax.random.normal(ks[5], (1, H, 1, HD), jnp.float32) * s, 'W_proj': jax.random.normal(ks[6], (D, D), jnp.float32) * s, 'b_proj': jnp.zeros((D,), jnp.float32)}
    _L0_cond_all = _L0_cond_setup()
    _L0_cond_in = {k: v for k, v in _L0_cond_all.items() if k in ('W_q', 'b_q', 'W_kv', 'b_kv', 'no_op_k', 'no_op_v', 'W_proj', 'b_proj')}
    del _L0_cond_all

    def _L1_cond_setup():
        import jax, jax.numpy as jnp
        import numpy as np
        TOP_K = 2
        N_EXPERTS = 8
        N_SHARED = 1
        EPS = 1e-09
        key = jax.random.key(seed)
        ks = jax.random.split(key, 10)
        B, T, d = (2, 512, 256)
        h_s, h_r, E = (512, 128, N_EXPERTS)
        return {'x': jax.random.normal(ks[0], (B, T, d), jnp.float32), 't_emb': jax.random.normal(ks[1], (B, d), jnp.float32), 'router_w': jax.random.normal(ks[2], (E, d), jnp.float32) * 0.01, 'router_t_w': jax.random.normal(ks[3], (E, d), jnp.float32) * 0.01, 'router_bias': jnp.zeros((E,), jnp.float32), 'sw1': jax.random.normal(ks[4], (h_s, d), jnp.float32) * 0.02, 'sw3': jax.random.normal(ks[5], (h_s, d), jnp.float32) * 0.02, 'sw2': jax.random.normal(ks[6], (d, h_s), jnp.float32) * 0.02, 'rw1': jax.random.normal(ks[7], (E, h_r, d), jnp.float32) * 0.02, 'rw2': jax.random.normal(ks[8], (E, d, h_r), jnp.float32) * 0.02}
    _L1_cond_all = _L1_cond_setup()
    _L1_cond_in = {k: v for k, v in _L1_cond_all.items() if k in ('router_w', 'router_t_w', 'router_bias', 'sw1', 'sw3', 'sw2', 'rw1', 'rw2')}
    del _L1_cond_all

    def _L2_cond_setup():
        import jax, jax.numpy as jnp
        import numpy as np
        B, N, D, C = (32, 64, 256, 256)
        key = jax.random.key(seed)
        k1, k2, k3, k4 = jax.random.split(key, 4)
        scale = 1.0 / np.sqrt(D)
        return {'encoded_utterance': jax.random.normal(k1, (B, D), dtype=jnp.float32), 'element_embeddings': jax.random.normal(k2, (B, N, D), dtype=jnp.float32), 'weight_matrix': jax.random.normal(k3, (2 * D, C), dtype=jnp.float32) * scale, 'W_proj': jax.random.normal(k4, (D, D), dtype=jnp.float32) * scale, 'b_proj': jnp.zeros((D,), dtype=jnp.float32)}
    _L2_cond_all = _L2_cond_setup()
    _L2_cond_in = {k: v for k, v in _L2_cond_all.items() if k in ('weight_matrix', 'W_proj', 'b_proj')}
    del _L2_cond_all

    def _L3_cond_setup():
        import jax, jax.numpy as jnp
        import numpy as np
        import math
        D = 256
        H = 256
        key = jax.random.key(seed)
        k1, k2, k3, k4 = jax.random.split(key, 4)
        x = jax.random.normal(k1, (64, 128, D), dtype=jnp.float32)
        h0 = jax.random.normal(k2, (64, H), dtype=jnp.float32)
        Wx = jax.random.normal(k3, (D, 4 * H), dtype=jnp.float32) / math.sqrt(D)
        Wh = jax.random.normal(k4, (H, 4 * H), dtype=jnp.float32) / math.sqrt(H)
        b = jnp.zeros((4 * H,), dtype=jnp.float32)
        return {'x': x, 'h0': h0, 'Wx': Wx, 'Wh': Wh, 'b': b}
    _L3_cond_all = _L3_cond_setup()
    _L3_cond_in = {k: v for k, v in _L3_cond_all.items() if k in ('Wx', 'Wh', 'b')}
    del _L3_cond_all
    return {'x': x, 'cond_1024': cond_1024, 'L0_cond_W_q': _L0_cond_in['W_q'], 'L0_cond_b_q': _L0_cond_in['b_q'], 'L0_cond_W_kv': _L0_cond_in['W_kv'], 'L0_cond_b_kv': _L0_cond_in['b_kv'], 'L0_cond_no_op_k': _L0_cond_in['no_op_k'], 'L0_cond_no_op_v': _L0_cond_in['no_op_v'], 'L0_cond_W_proj': _L0_cond_in['W_proj'], 'L0_cond_b_proj': _L0_cond_in['b_proj'], 'L1_cond_router_w': _L1_cond_in['router_w'], 'L1_cond_router_t_w': _L1_cond_in['router_t_w'], 'L1_cond_router_bias': _L1_cond_in['router_bias'], 'L1_cond_sw1': _L1_cond_in['sw1'], 'L1_cond_sw3': _L1_cond_in['sw3'], 'L1_cond_sw2': _L1_cond_in['sw2'], 'L1_cond_rw1': _L1_cond_in['rw1'], 'L1_cond_rw2': _L1_cond_in['rw2'], 'L2_cond_weight_matrix': _L2_cond_in['weight_matrix'], 'L2_cond_W_proj': _L2_cond_in['W_proj'], 'L2_cond_b_proj': _L2_cond_in['b_proj'], 'L3_cond_Wx': _L3_cond_in['Wx'], 'L3_cond_Wh': _L3_cond_in['Wh'], 'L3_cond_b': _L3_cond_in['b']}

def reference(x, cond_1024, L0_cond_W_q, L0_cond_b_q, L0_cond_W_kv, L0_cond_b_kv, L0_cond_no_op_k, L0_cond_no_op_v, L0_cond_W_proj, L0_cond_b_proj, L1_cond_router_w, L1_cond_router_t_w, L1_cond_router_bias, L1_cond_sw1, L1_cond_sw3, L1_cond_sw2, L1_cond_rw1, L1_cond_rw2, L2_cond_weight_matrix, L2_cond_W_proj, L2_cond_b_proj, L3_cond_Wx, L3_cond_Wh, L3_cond_b):
    import jax
    import jax.numpy as jnp

    def _L0_cond_ref(hidden_states, activation, W_q, b_q, W_kv, b_kv, no_op_k, no_op_v, W_proj, b_proj):
        import jax, jax.numpy as jnp
        import numpy as np
        B, S, D = (8, 1024, 256)
        H = 16
        HD = D // H
        ACT_DIM = 256
        b = hidden_states.shape[0]
        q = hidden_states @ W_q + b_q
        q = q.reshape(b, -1, H, HD).transpose(0, 2, 1, 3)
        kv = activation @ W_kv + b_kv
        k1, v1 = (kv[:, :D], kv[:, D:])
        k1 = k1.reshape(b, 1, H, HD).transpose(0, 2, 1, 3)
        v1 = v1.reshape(b, 1, H, HD).transpose(0, 2, 1, 3)
        k = jnp.concatenate([jnp.broadcast_to(no_op_k, (b, H, 1, HD)), k1], axis=2)
        v = jnp.concatenate([jnp.broadcast_to(no_op_v, (b, H, 1, HD)), v1], axis=2)
        scores = jnp.einsum('bhsd,bhkd->bhsk', q, k)
        w = jax.nn.softmax(scores, axis=-1)
        attn = jnp.einsum('bhsk,bhkd->bhsd', w, v)
        attn = attn.transpose(0, 2, 1, 3).reshape(b, -1, D)
        out = attn @ W_proj + b_proj
        return out

    def _L1_cond_ref(x, t_emb, router_w, router_t_w, router_bias, sw1, sw3, sw2, rw1, rw2):
        import jax, jax.numpy as jnp
        import numpy as np
        TOP_K = 2
        N_EXPERTS = 8
        N_SHARED = 1
        EPS = 1e-09
        B, T, C = x.shape
        N = B * T
        x_flat = x.reshape(N, C)
        shared_out = jnp.einsum('nh,dh->nd', jax.nn.silu(x_flat @ sw1.T) * (x_flat @ sw3.T), sw2)
        t_bias = t_emb @ router_t_w.T
        t_bias_flat = jnp.broadcast_to(t_bias[:, None, :], (B, T, N_EXPERTS)).reshape(N, N_EXPERTS)
        s = jax.nn.sigmoid((x_flat @ router_w.T + t_bias_flat).astype(jnp.float32))
        sel_scores = s + router_bias
        _, topk_idx = jax.lax.top_k(sel_scores, TOP_K)
        s_sel = jnp.take_along_axis(s, topk_idx, axis=1)
        denom = jnp.sum(s_sel, axis=1, keepdims=True)
        gates = jnp.where(denom > EPS, s_sel / (denom + EPS), 1.0 / TOP_K).astype(x.dtype)
        combine = jnp.sum(gates[:, :, None] * jax.nn.one_hot(topk_idx, N_EXPERTS, dtype=x.dtype), axis=1)
        H = jax.nn.gelu(jnp.einsum('nd,ehd->enh', x_flat, rw1), approximate=False)
        O = jnp.einsum('enh,edh->end', H, rw2)
        routed_out = jnp.einsum('end,ne->nd', O, combine)
        out = (shared_out + routed_out) / (N_SHARED + TOP_K)
        return out.reshape(B, T, C)

    def _L2_cond_ref(encoded_utterance, element_embeddings, weight_matrix, W_proj, b_proj):
        import jax, jax.numpy as jnp
        import numpy as np
        B, N, D, C = (32, 64, 256, 256)
        u = jax.nn.gelu(encoded_utterance @ W_proj + b_proj, approximate=False)
        W_u, W_e = (weight_matrix[:D], weight_matrix[D:])
        logits = (u @ W_u)[:, None, :] + jnp.einsum('bnd,dc->bnc', element_embeddings, W_e)
        return logits

    def _L3_cond_ref(x, h0, Wx, Wh, b):
        import jax, jax.numpy as jnp
        import numpy as np
        import math
        D = 256
        H = 256
        xz = jnp.einsum('ntd,dk->ntk', x, Wx) + b
        c0 = jnp.zeros_like(h0)

        def step(carry, xz_t):
            prev_h, prev_c = carry
            z = xz_t + prev_h @ Wh
            ai, af, ao, ag = jnp.split(z, 4, axis=1)
            i = jax.nn.sigmoid(ai)
            f = jax.nn.sigmoid(af)
            o = jax.nn.sigmoid(ao)
            g = jnp.tanh(ag)
            next_c = f * prev_c + i * g
            next_h = o * jnp.tanh(next_c)
            return ((next_h, next_c), next_h)
        _, hs = jax.lax.scan(step, (h0, c0), jnp.swapaxes(xz, 0, 1))
        return jnp.swapaxes(hs, 0, 1)
    x = x + _L0_cond_ref(x, cond_1024, L0_cond_W_q, L0_cond_b_q, L0_cond_W_kv, L0_cond_b_kv, L0_cond_no_op_k, L0_cond_no_op_v, L0_cond_W_proj, L0_cond_b_proj)
    x = x + _L1_cond_ref(x, cond_1024, L1_cond_router_w, L1_cond_router_t_w, L1_cond_router_bias, L1_cond_sw1, L1_cond_sw3, L1_cond_sw2, L1_cond_rw1, L1_cond_rw2)
    x = x + _L2_cond_ref(cond_1024, x, L2_cond_weight_matrix, L2_cond_W_proj, L2_cond_b_proj)
    x = x + _L3_cond_ref(x, cond_1024, L3_cond_Wx, L3_cond_Wh, L3_cond_b)
    return x

_drawn_inputs = setup_inputs


def setup_inputs(seed=0):
    import zlib

    import numpy as np

    out = dict(_drawn_inputs(seed))
    spreads = {'L0_cond_b_q': (0.0, 0.8),
     'L0_cond_b_kv': (0.0, 0.498),
     'L0_cond_b_proj': (0.0, 0.1),
     'L1_cond_router_bias': (0.0, 0.8),
     'L2_cond_b_proj': (0.0, 0.757),
     'L3_cond_b': (0.0, 2.0)}
    factors = {'L0_cond_W_q': 5.661,
     'L0_cond_no_op_k': 8.0,
     'L0_cond_no_op_v': 8.0,
     'L1_cond_router_w': 8.0,
     'L1_cond_router_t_w': 8.0,
     'L1_cond_sw1': 7.652,
     'L1_cond_sw3': 7.581,
     'L1_cond_sw2': 7.537,
     'L1_cond_rw1': 6.687,
     'L1_cond_rw2': 6.581,
     'L3_cond_Wh': 6.77}
    for name, (base, spread) in spreads.items():
        noise = np.random.default_rng([zlib.crc32(name.encode()), seed]).standard_normal(out[name].shape)
        drawn = base * np.exp(spread * noise) if base else spread * noise
        out[name] = jnp.asarray(drawn.astype(out[name].dtype))
    for name, factor in factors.items():
        out[name] = (out[name] * factor).astype(out[name].dtype)
    return out
```

```python
from contextlib import ExitStack

import concourse.bass as bass
from concourse import mybir

F32 = mybir.dt.float32
ALU = mybir.AluOpType
ACT = mybir.ActivationFunctionType
AX = mybir.AxisListType

P = 128
B, T, D = 2, 1024, 256
C = D // P
HEADS = 16
HS = 512
MS = HS // P
E = 8
G4 = 4 * D
TOP_K = 2
EPS = 1e-9

CT = 256
CHUNKS = T // CT
NT = B * CT
Q = NT // P
HALVES = CT // P
XZ_COLS = 512
NXZ = Q * (G4 // XZ_COLS)

U = 8
ITERS = T // U
HU = U // 2
J = 4
HC = D // J
GI, GF, GO, GC = 0, 1, 2, 3
STORES = 8

SMALL = {}


def _pack_small():
    at = 0
    for name, width in (("cond", C * B), ("b_q", C), ("b_kv", 2 * C), ("no_k", C), ("no_v", C),
                        ("b_proj", C), ("b_proj2", C), ("router", C * E), ("router_t", C * E),
                        ("router_bias", E), ("head", C * HEADS), ("before", E * E), ("ident", 16)):
        SMALL[name] = (at, at + width)
        at += width
    return at


N_SMALL = _pack_small()


def cond_stack_kernel(nc, x, small, wkv, wq, wproj, sw1, sw3, sw2, rw1, rw2, wu, we, wproj2, wx, wh,
                      bias_z, y):
    ctx = ExitStack()
    with ctx:
        def sb(name, shape):
            return ctx.enter_context(nc.sbuf_tensor(name, shape, F32))

        def sem(name):
            return ctx.enter_context(nc.semaphore(name))

        xz_dram = nc.dram_tensor("xz_scratch", (B, T, G4), F32).ap()
        comb_dram = nc.dram_tensor("comb_scratch", (CHUNKS, NT * E), F32).ap()

        small_sb = sb("small_sb", [P, N_SMALL])
        wkv_sb = sb("wkv_sb", [P, C, 2 * D])
        wq_sb = sb("wq_sb", [P, C, D])
        wproj_sb = sb("wproj_sb", [P, C, D])
        sw1_sb = sb("sw1_sb", [P, C, HS])
        sw3_sb = sb("sw3_sb", [P, C, HS])
        sw2_sb = sb("sw2_sb", [P, MS, D])
        rw1_sb = sb("rw1_sb", [P, E, C, P])
        rw2_sb = sb("rw2_sb", [P, E, D])
        wu_sb = sb("wu_sb", [P, C, D])
        we_sb = sb("we_sb", [P, C, D])
        wproj2_sb = sb("wproj2_sb", [P, C, D])
        wx_sb = sb("wx_sb", [P, C, G4])
        wh_sb = sb("wh_sb", [P, C, G4])
        bias_z_sb = sb("bias_z_sb", [P, G4])

        def part(name, pattern=None, **kw):
            ap = small_sb[:, SMALL[name][0]:SMALL[name][1]]
            return ap.rearrange(pattern, **kw) if pattern else ap

        cond = part("cond", "p (c b) -> p c b", c=C)
        b_q = part("b_q")
        b_kv = part("b_kv")
        no_k, no_v = part("no_k"), part("no_v")
        b_proj, b_proj2 = part("b_proj"), part("b_proj2")
        router = part("router", "p (c e) -> p c e", c=C)
        router_t = part("router_t", "p (c e) -> p c e", c=C)
        router_bias = part("router_bias")
        head = part("head", "p (c h) -> p c h", c=C)
        before = part("before", "p (e f) -> p e f", e=E)
        ident = part("ident")

        stream = sb("stream", [P, C, B, T])

        kv = sb("kv", [P, 2 * C, B])
        k_diff = sb("k_diff", [P, C, B])
        v_diff = sb("v_diff", [P, C, B])
        k_heads = sb("k_heads", [P, C, B, HEADS])
        v_heads = sb("v_heads", [P, C, B, HEADS])
        score_w = sb("score_w", [P, C, B, HEADS])
        score_b = sb("score_b", [HEADS, B])
        value_w = sb("value_w", [HEADS, B, D])
        attn_b = sb("attn_b", [P, C])
        cond_rep = sb("cond_rep", [P, C, B, P])
        u_act = sb("u_act", [P, C, B])
        cond_out = sb("cond_out", [P, C, B])

        w1 = sb("w1", [HEADS, B, CT])
        x1 = sb("x1", [P, C, NT])
        x2 = sb("x2", [P, C, NT])
        x3 = sb("x3", [P, C, NT])
        s_all = sb("s_all", [P, Q, E])
        sel = sb("sel", [P, Q, E])
        beats = sb("beats", [P, Q, E, E])
        ties = sb("ties", [P, Q, E, E])
        rank = sb("rank", [P, Q, E])
        s_top = sb("s_top", [P, Q, E])
        top = sb("top", [P, Q, E])
        den = sb("den", [P, Q])
        den_eps = sb("den_eps", [P, Q])
        den_inv = sb("den_inv", [P, Q])
        den_ok = sb("den_ok", [P, Q])
        inv_ok = sb("inv_ok", [P, Q])
        half_bad = sb("half_bad", [P, Q])
        comb_a = sb("comb_a", [P, Q, E])
        comb_b = sb("comb_b", [P, Q, E])
        comb = sb("comb", [P, Q, E])
        comb_all = sb("comb_all", [P, NT, E])
        sig = sb("sig", [P, 2, NT])
        gated = sb("gated", [P, 2, NT])
        shared = sb("shared", [P, MS, NT])
        expert = sb("expert", [P, E, NT])
        xz_sb = sb("xz_sb", [P, Q, G4])

        staged = sb("staged", [P, 2, 4, D])
        h_ring = sb("h_ring", [P, U, C, B])
        if_act = sb("if_act", [P, 2, 2, C * B, 2])
        o_act = sb("o_act", [P, 2, C * B])

        bank = [ctx.enter_context(nc.psum_tensor(f"bank{n}", [P, 512], F32)) for n in range(8)]

        t_if_b = bank[3][:, 0:3 * HC].rearrange("p (g c r) -> p g c r", g=3, r=32)
        t_c_b = bank[4][:, 0:HC].rearrange("p (c r) -> p c r", r=32)
        cell_b = bank[5][:, 0:4 * C * B].rearrange("p (v q k) -> p v q k", v=2, k=2)
        g_pairs = bank[6][:, 0:4 * C * B].rearrange("p (v q k) -> p v q k", v=2, k=2)
        c_tanh = bank[6][:, 4 * C * B:6 * C * B].rearrange("p (v q) -> p v q", v=2)

        small_in = sem("small_in")
        x_in = sem("x_in")
        w_in = {n: sem(f"{n}_in") for n in ("wkv", "wq", "wproj", "sw1", "sw3", "sw2", "rw1", "rw2", "wu",
                                            "we", "wproj2", "wx", "wh", "bias_z")}
        kv_made = sem("kv_made")
        kv_out = sem("kv_out")
        diff_made = sem("diff_made")
        heads_made = sem("heads_made")
        u_made = sem("u_made")
        u_out = sem("u_out")
        setup_made = sem("setup_made")
        setup_out = sem("setup_out")
        rep_made = sem("rep_made")
        d_made = sem("d_made")
        w1_out = sem("w1_out")
        attn_made = sem("attn_made")
        x1_out = sem("x1_out")
        route_made = sem("route_made")
        s_out = sem("s_out")
        top_step = sem("top_step")
        comb_out = sem("comb_out")
        comb_stored = sem("comb_stored")
        comb_in = sem("comb_in")
        up_made = sem("up_made")
        sig_out = sem("sig_out")
        gated_out = sem("gated_out")
        shared_out = sem("shared_out")
        hid_made = sem("hid_made")
        gelu_out = sem("gelu_out")
        expert_out = sem("expert_out")
        moe_made = sem("moe_made")
        x2_out = sem("x2_out")
        lin_made = sem("lin_made")
        x3_out = sem("x3_out")
        x3_kept = sem("x3_kept")
        xz_made = sem("xz_made")
        xz_out = sem("xz_out")
        xz_stored = [sem(f"xz_stored{q}") for q in range(Q)]
        z_if = sem("z_if")
        z_c = sem("z_c")
        z_o = sem("z_o")
        t_if = sem("t_if")
        t_c = sem("t_c")
        t_o = sem("t_o")
        a_if = sem("a_if")
        a_c = sem("a_c")
        a_o = sem("a_o")
        kept = sem("kept")
        cell = sem("cell")
        cell_tanh = sem("cell_tanh")
        hid = sem("hid")
        staged_clear = sem("staged_clear")
        staged_in = [sem(f"staged_in{n}") for n in range(2)]
        staged_used = [sem(f"staged_used{n}") for n in range(2)]
        added = sem("added")
        y_stored = sem("y_stored")

        block = ctx.enter_context(nc.Block())

        @block.sync
        def _(sp):
            sp.dma_start(small_sb[:, :], small).then_inc(small_in, 16)
            for name, dst, src in (("wkv", wkv_sb, wkv), ("wq", wq_sb, wq), ("wproj", wproj_sb, wproj),
                                   ("sw1", sw1_sb, sw1), ("sw3", sw3_sb, sw3), ("rw1", rw1_sb, rw1),
                                   ("sw2", sw2_sb, sw2), ("rw2", rw2_sb, rw2), ("we", we_sb, we),
                                   ("wx", wx_sb, wx), ("bias_z", bias_z_sb, bias_z), ("wh", wh_sb, wh)):
                sp.dma_start(dst[:], src).then_inc(w_in[name], 16)

            with sp.Fori(0, CHUNKS) as i:
                sp.wait_ge(comb_out, i + 1)
                sp.dma_start(comb_dram[bass.ds(i, 1), :].rearrange("a (q p e) -> p (a q) e", q=Q, e=E),
                             comb[:, :, :]).then_inc(comb_stored, 16)
                sp.wait_ge(comb_stored, i * 16 + 16)
                sp.dma_start(comb_all[:, :, :].rearrange("p n e -> p (n e)"),
                             comb_dram[bass.ds(i, 1), :].partition_broadcast(P).rearrange("p a n -> p (a n)")
                             ).then_inc(comb_in, 16)
                for q in range(Q):
                    b, half = q // HALVES, q % HALVES
                    sp.wait_ge(xz_out, i * NXZ + 2 * (q + 1))
                    sp.dma_start(xz_dram[b, bass.ds(i * CT + half * P, P), :],
                                 xz_sb[:, q, :]).then_inc(xz_stored[q], 16)

            def stage(step, n):
                for b in range(B):
                    sp.dma_start(staged[b * HU:(b + 1) * HU, n, :, :].rearrange("p g d -> p (g d)"),
                                 xz_dram[b, bass.ds(step, HU), :]).then_inc(staged_in[n], 16)

            for q in range(Q):
                sp.wait_ge(xz_stored[q], 16 * (CHUNKS + 1))
            sp.wait_ge(staged_clear, 1)
            for n in range(2):
                stage(n * HU, n)
            per_store = ITERS // STORES

            def store(at, first):
                sp.wait_ge(added, first + 1)
                sp.dma_start(y[:, :, :, bass.ds(at, T // STORES)],
                             stream[:, :, :, bass.ds(at, T // STORES)]).then_inc(y_stored, 16)

            with sp.Fori(0, STORES - 1) as o:
                with sp.Fori(0, per_store) as k:
                    for n in range(2):
                        sp.wait_ge(staged_used[n], o * per_store + k + 1)
                        stage((o * per_store + k + 1) * U + n * HU, n)
                store(o * (T // STORES), (o + 1) * per_store)
            with sp.Fori(0, per_store - 1) as k:
                for n in range(2):
                    sp.wait_ge(staged_used[n], k + (STORES - 1) * per_store + 1)
                    stage((k + (STORES - 1) * per_store + 1) * U + n * HU, n)
            store((STORES - 1) * (T // STORES), ITERS)
            sp.wait_ge(y_stored, 16 * STORES)

        @block.gpsimd
        def _(pool):
            pool.sem_inc(x3_kept, 1)
            for q in range(Q):
                pool.sem_inc(xz_stored[q], 16)
            pool.sem_inc(added, 1)
            pool.memset(staged[:, :, :, :], 0.0).then_inc(staged_clear, 1)
            with pool.Fori(0, CHUNKS) as i:
                pool.wait_ge(x3_out, i * (C * B) + C * B)
                pool.tensor_copy(stream[:, :, :, bass.ds(i * CT, CT)],
                                 x3[:, :, :].rearrange("p c (b t) -> p c b t", b=B)).then_inc(x3_kept, 1)
            with pool.Fori(0, ITERS) as i:
                pool.wait_ge(hid, i * U + U + 1)
                out = stream[:, :, :, bass.ds(i * U, U)].rearrange("p c b t -> p (c b) t")
                pool.tensor_tensor(out, out, h_ring[:, :, :, :].rearrange("p u c b -> p (c b) u"),
                                   ALU.add).then_inc(added, 1)

        @block.scalar
        def _(act):
            act.dma_start(wproj2_sb[:], wproj2).then_inc(w_in["wproj2"], 16)
            act.dma_start(wu_sb[:], wu).then_inc(w_in["wu"], 16)
            act.dma_start(stream[:, :, :, :], x).then_inc(x_in, 16)
            act.wait_ge(small_in, 16)
            act.wait_ge(u_made, 1)
            for m in range(C):
                nc.scalar.activation(u_act[:, m, :], bank[4][:, m * B:(m + 1) * B], ACT.Gelu,
                                     bias=b_proj2[:, m:m + 1]).then_inc(u_out, 1)
            act.wait_ge(setup_out, 5)
            with act.Fori(0, CHUNKS) as i:
                act.wait_ge(d_made, i + 1)
                for b in range(B):
                    nc.scalar.activation(w1[:, b, :], bank[0][0:HEADS, b * CT:(b + 1) * CT], ACT.Sigmoid,
                                         bias=score_b[:, b:b + 1]).then_inc(w1_out, 1)
                act.wait_ge(route_made, i + 1)
                nc.scalar.activation(s_all[:, :, :].rearrange("p q e -> p (q e)"), bank[3][:, 0:Q * E],
                                     ACT.Sigmoid).then_inc(s_out, 1)
                for m in range(MS):
                    act.wait_ge(up_made, i * MS + m + 1)
                    if m >= 2:
                        act.wait_ge(gated_out, i * MS + m - 1)
                    nc.scalar.activation(sig[:, m % 2, :], bank[4 + 2 * (m % 2)][:, :],
                                         ACT.Sigmoid).then_inc(sig_out, 1)
                for e in range(E):
                    act.wait_ge(hid_made, i * E + e + 1)
                    nc.scalar.activation(expert[:, e, :], bank[e % 4][:, :], ACT.Gelu).then_inc(gelu_out, 1)

            act.preload_act_table_set("sigmoid_and_others")
            with act.Fori(0, ITERS) as i:
                count = [act.snap(i * U + u + 1) for u in range(U + 1)]
                for u in range(U):
                    par = u % 2
                    act.wait_ge(t_if, count[u + 1])
                    nc.scalar.activation(if_act[:, par, :, :, 0], t_if_b[:, 0:2, :, 0:B],
                                         ACT.Sigmoid).then_inc(a_if, 1)
                    act.wait_ge(t_c, count[u + 1])
                    nc.scalar.activation(g_pairs[:, par, :, 1], t_c_b[:, :, 0:B], ACT.Tanh).then_inc(a_c, 1)
                    act.wait_ge(t_o, count[u + 1])
                    nc.scalar.activation(o_act[:, par, :], t_if_b[:, 2, :, 0:B], ACT.Sigmoid).then_inc(a_o, 1)
                    act.wait_ge(cell, count[u + 1])
                    nc.scalar.activation(c_tanh[:, par, :], cell_b[:, par, :, 1],
                                         ACT.Tanh).then_inc(cell_tanh, 1)

        @block.vector
        def _(dve):
            def pairs(ap):
                return ap.unsqueeze(2).to_broadcast([P, C, B])

            dve.wait_ge(small_in, 16)
            nc.vector.tensor_copy(cond_rep[:, :, :, :],
                                  cond.unsqueeze(3).to_broadcast([P, C, B, P])).then_inc(rep_made, 1)
            dve.wait_ge(kv_made, 1)
            nc.vector.tensor_tensor(kv[:, :, :], bank[0][:, 0:2 * C * B].rearrange("p (m b) -> p m b", b=B),
                                    b_kv.unsqueeze(2).to_broadcast([P, 2 * C, B]), ALU.add).then_inc(kv_out, 1)
            dve.wait_ge(kv_out, 1)
            nc.vector.tensor_tensor(k_diff[:, :, :], kv[:, 0:C, :], pairs(no_k), ALU.subtract).then_inc(diff_made, 1)
            nc.vector.tensor_tensor(v_diff[:, :, :], kv[:, C:2 * C, :], pairs(no_v),
                                    ALU.subtract).then_inc(diff_made, 1)
            dve.wait_ge(diff_made, 2)
            for dst, src in ((k_heads, k_diff), (v_heads, v_diff)):
                for m in range(C):
                    nc.vector.tensor_tensor(dst[:, m, :, :],
                                            head[:, m, :].unsqueeze(1).to_broadcast([P, B, HEADS]),
                                            src[:, m, :].unsqueeze(2).to_broadcast([P, B, HEADS]),
                                            ALU.mult).then_inc(heads_made, 1)
            dve.wait_ge(setup_made, 1)
            nc.vector.tensor_copy(score_w[:, :, :, :].rearrange("p c b h -> p (c b h)"),
                                  bank[1][:, 0:C * B * HEADS]).then_inc(setup_out, 1)
            dve.wait_ge(setup_made, 2)
            nc.vector.tensor_copy(score_b[:, :], bank[2][0:HEADS, 0:B]).then_inc(setup_out, 1)
            nc.vector.tensor_tensor(attn_b[:, :], bank[2][:, 8:8 + C], b_proj, ALU.add).then_inc(setup_out, 1)
            dve.wait_ge(setup_made, 3)
            nc.vector.tensor_copy(value_w[:, :, :].rearrange("h b d -> h (b d)"),
                                  bank[3][0:HEADS, :]).then_inc(setup_out, 1)
            dve.wait_ge(setup_made, 4)
            nc.vector.tensor_copy(cond_out[:, :, :].rearrange("p c b -> p (c b)"),
                                  bank[5][:, 0:C * B]).then_inc(setup_out, 1)
            dve.wait_ge(setup_out, 5)
            dve.wait_ge(x_in, 16)

            with dve.Fori(0, CHUNKS) as i:
                for c in range(C):
                    dve.wait_ge(attn_made, i * C + c + 1)
                    nc.vector.scalar_tensor_tensor(
                        out=x1[:, c, :].rearrange("p (b t) -> p b t", b=B),
                        in0=bank[1 + c][:, :].rearrange("p (b t) -> p b t", b=B), scalar=attn_b[:, c:c + 1],
                        in1=stream[:, c, :, bass.ds(i * CT, CT)], op0=ALU.add, op1=ALU.add).then_inc(x1_out, 1)

                steps = 11
                done = [0]

                def step(ins):
                    done[0] += 1
                    ins.then_inc(top_step, 1)
                    dve.wait_ge(top_step, i * steps + done[0])

                rivals = sel[:, :, :].unsqueeze(2).to_broadcast([P, Q, E, E])
                own = sel[:, :, :].unsqueeze(3).to_broadcast([P, Q, E, E])
                dve.wait_ge(s_out, i + 1)
                step(nc.vector.tensor_tensor(sel[:, :, :], s_all[:, :, :],
                                             router_bias.unsqueeze(1).to_broadcast([P, Q, E]), ALU.add))
                nc.vector.tensor_tensor(beats[:, :, :, :], rivals, own, ALU.is_gt)
                step(nc.vector.tensor_tensor(ties[:, :, :, :], rivals, own, ALU.is_equal))
                step(nc.vector.tensor_tensor(ties[:, :, :, :], ties[:, :, :, :],
                                             before.unsqueeze(1).to_broadcast([P, Q, E, E]), ALU.mult))
                step(nc.vector.tensor_tensor(beats[:, :, :, :], beats[:, :, :, :], ties[:, :, :, :], ALU.add))
                step(nc.vector.tensor_reduce(rank[:, :, :], beats[:, :, :, :], AX.X, ALU.add))
                nc.vector.tensor_scalar(top[:, :, :], rank[:, :, :], float(TOP_K), None, ALU.is_lt)
                step(nc.vector.scalar_tensor_tensor(out=s_top[:, :, :], in0=rank[:, :, :], scalar=float(TOP_K),
                                                    in1=s_all[:, :, :], op0=ALU.is_lt, op1=ALU.mult))
                step(nc.vector.tensor_reduce(den[:, :], s_top[:, :, :], AX.X, ALU.add))
                nc.vector.tensor_scalar(den_ok[:, :], den[:, :], EPS, None, ALU.is_gt)
                step(nc.vector.tensor_scalar(den_eps[:, :], den[:, :], EPS, None, ALU.add))
                nc.vector.tensor_scalar(half_bad[:, :], den_ok[:, :], -1.0 / TOP_K, 1.0 / TOP_K, ALU.mult, ALU.add)
                step(nc.vector.reciprocal(den_inv[:, :], den_eps[:, :]))
                nc.vector.tensor_tensor(comb_b[:, :, :], top[:, :, :],
                                        half_bad[:, :].unsqueeze(2).to_broadcast([P, Q, E]), ALU.mult)
                step(nc.vector.tensor_tensor(inv_ok[:, :], den_inv[:, :], den_ok[:, :], ALU.mult))
                step(nc.vector.tensor_tensor(comb_a[:, :, :], s_top[:, :, :],
                                             inv_ok[:, :].unsqueeze(2).to_broadcast([P, Q, E]), ALU.mult))
                nc.vector.tensor_tensor(comb[:, :, :], comb_a[:, :, :], comb_b[:, :, :],
                                        ALU.add).then_inc(comb_out, 1)
                assert done[0] == steps

                for m in range(MS):
                    pair = 4 + 2 * (m % 2)
                    dve.wait_ge(sig_out, i * MS + m + 1)
                    nc.vector.tensor_tensor(gated[:, m % 2, :], sig[:, m % 2, :], bank[pair][:, :],
                                            ALU.mult).then_inc(gated_out, 1)
                    dve.wait_ge(gated_out, i * MS + m + 1)
                    nc.vector.tensor_tensor(shared[:, m, :], gated[:, m % 2, :], bank[pair + 1][:, :],
                                            ALU.mult).then_inc(shared_out, 1)
                dve.wait_ge(comb_in, i * 16 + 16)
                for e in range(E):
                    dve.wait_ge(gelu_out, i * E + e + 1)
                    nc.vector.tensor_tensor(expert[:, e, :], expert[:, e, :], comb_all[:, :, e],
                                            ALU.mult).then_inc(expert_out, 1)
                for c in range(C):
                    dve.wait_ge(moe_made, i * C + c + 1)
                    nc.vector.scalar_tensor_tensor(out=x2[:, c, :], in0=bank[4 + c][:, :],
                                                   scalar=1.0 / (1 + TOP_K), in1=x1[:, c, :], op0=ALU.mult,
                                                   op1=ALU.add).then_inc(x2_out, 1)
                dve.wait_ge(x3_kept, i + 1)
                for c in range(C):
                    dve.wait_ge(lin_made, i * C + c + 1)
                    for b in range(B):
                        cols = slice(b * CT, (b + 1) * CT)
                        nc.vector.scalar_tensor_tensor(out=x3[:, c, cols], in0=bank[6 + c][:, cols],
                                                       scalar=cond_out[:, c, b:b + 1], in1=x2[:, c, cols],
                                                       op0=ALU.add, op1=ALU.add).then_inc(x3_out, 1)
                for n in range(NXZ):
                    q, g = n // 2, n % 2
                    cols = slice(g * XZ_COLS, (g + 1) * XZ_COLS)
                    if g == 0:
                        dve.wait_ge(xz_stored[q], i * 16 + 16)
                    dve.wait_ge(xz_made, i * NXZ + n + 1)
                    nc.vector.tensor_tensor(xz_sb[:, q, cols], bank[n % 4][:, :], bias_z_sb[:, cols],
                                            ALU.add).then_inc(xz_out, 1)

            dve.wait_ge(xz_out, CHUNKS * NXZ)
            nc.vector.memset(bank[0][:, :], 0.0).then_inc(t_if, 1)
            nc.vector.memset(bank[1][:, :], 0.0).then_inc(t_c, 1)
            nc.vector.memset(bank[2][:, :], 0.0).then_inc(t_o, 1)
            nc.vector.memset(bank[6][:, 0:6 * C * B], 0.0)
            nc.vector.memset(bank[5][:, 0:4 * C * B], 0.0).then_inc(cell, 1)
            nc.vector.tensor_copy(h_ring[:, U - 1, :, :], cond).then_inc(hid, 1)
            with dve.Fori(0, ITERS) as i:
                added_count = dve.snap(i + 1)
                count = [dve.snap(i * U + u + 1) for u in range(U)]
                for u in range(U):
                    par, now = u % 2, count[u]
                    dve.wait_ge(z_if, now)
                    nc.vector.transpose(bank[3][:, 0:2 * HC], bank[0][:, 0:2 * HC]).then_inc(t_if, 1)
                    dve.wait_ge(z_c, now)
                    nc.vector.transpose(bank[4][:, 0:HC], bank[1][:, 0:HC]).then_inc(t_c, 1)
                    dve.wait_ge(a_if, now)
                    dve.wait_ge(cell, now)
                    nc.vector.tensor_tensor(if_act[:, par, 0, :, 1], if_act[:, par, 1, :, 0],
                                            cell_b[:, 1 - par, :, 1], ALU.mult).then_inc(kept, 1)
                    dve.wait_ge(z_o, now)
                    nc.vector.transpose(bank[3][:, 2 * HC:3 * HC], bank[2][:, 0:HC]).then_inc(t_o, 1)
                    dve.wait_ge(a_c, now)
                    dve.wait_ge(kept, now)
                    nc.vector.tensor_tensor_scan(cell_b[:, par, :, :].rearrange("p q k -> p (q k)"),
                                                 g_pairs[:, par, :, :].rearrange("p q k -> p (q k)"),
                                                 if_act[:, par, 0, :, :].rearrange("p q k -> p (q k)"), 0.0,
                                                 ALU.mult, ALU.add).then_inc(cell, 1)
                    dve.wait_ge(cell_tanh, now)
                    dve.wait_ge(a_o, now)
                    if u == 0:
                        dve.wait_ge(added, added_count)
                    nc.vector.tensor_tensor(h_ring[:, u, :, :].rearrange("p c b -> p (c b)"), o_act[:, par, :],
                                            c_tanh[:, par, :], ALU.mult).then_inc(hid, 1)

        @block.tensor
        def _(pe):
            pe.wait_ge(small_in, 16)
            pe.wait_ge(w_in["wproj2"], 16)
            for m in range(C):
                for c in range(C):
                    last = nc.tensor.matmul(bank[4][:, m * B:(m + 1) * B], wproj2_sb[:, c, m * P:(m + 1) * P],
                                            cond[:, c, :], start=(c == 0), stop=(c == C - 1))
            last.then_inc(u_made, 1)
            pe.wait_ge(w_in["wkv"], 16)
            for m in range(2 * C):
                for c in range(C):
                    last = nc.tensor.matmul(bank[0][:, m * B:(m + 1) * B], wkv_sb[:, c, m * P:(m + 1) * P],
                                            cond[:, c, :], start=(c == 0), stop=(c == C - 1))
            last.then_inc(kv_made, 1)
            pe.wait_ge(w_in["wq"], 16)
            pe.wait_ge(heads_made, 2 * C)
            for c in range(C):
                for m in range(C):
                    last = nc.tensor.matmul(bank[1][:, c * B * HEADS:(c + 1) * B * HEADS],
                                            wq_sb[:, m, c * P:(c + 1) * P],
                                            k_heads[:, m, :, :].rearrange("p b h -> p (b h)"),
                                            start=(m == 0), stop=(m == C - 1))
            last.then_inc(setup_made, 1)
            for b in range(B):
                for m in range(C):
                    nc.tensor.matmul(bank[2][0:HEADS, b:b + 1], k_heads[:, m, b, :], b_q[:, m:m + 1],
                                     start=(m == 0), stop=(m == C - 1))
            pe.wait_ge(w_in["wproj"], 16)
            for c in range(C):
                for m in range(C):
                    last = nc.tensor.matmul(bank[2][:, 8 + c:9 + c], wproj_sb[:, m, c * P:(c + 1) * P],
                                            no_v[:, m:m + 1], start=(m == 0), stop=(m == C - 1))
            last.then_inc(setup_made, 1)
            for b in range(B):
                for m in range(C):
                    last = nc.tensor.matmul(bank[3][0:HEADS, b * D:(b + 1) * D], v_heads[:, m, b, :],
                                            wproj_sb[:, m, :], start=(m == 0), stop=(m == C - 1))
            last.then_inc(setup_made, 1)
            pe.wait_ge(w_in["wu"], 16)
            pe.wait_ge(u_out, C)
            for c in range(C):
                for m in range(C):
                    last = nc.tensor.matmul(bank[5][:, c * B:(c + 1) * B], wu_sb[:, m, c * P:(c + 1) * P],
                                            u_act[:, m, :], start=(m == 0), stop=(m == C - 1))
            last.then_inc(setup_made, 1)
            pe.wait_ge(setup_out, 5)
            pe.wait_ge(rep_made, 1)
            pe.wait_ge(x_in, 16)

            with pe.Fori(0, CHUNKS) as i:
                for b in range(B):
                    for c in range(C):
                        last = nc.tensor.matmul(bank[0][0:HEADS, b * CT:(b + 1) * CT], score_w[:, c, b, :],
                                                stream[:, c, b, bass.ds(i * CT, CT)],
                                                start=(c == 0), stop=(c == C - 1))
                last.then_inc(d_made, 1)
                pe.wait_ge(w1_out, i * B + B)
                for c in range(C):
                    for b in range(B):
                        last = nc.tensor.matmul(bank[1 + c][:, b * CT:(b + 1) * CT],
                                                value_w[:, b, c * P:(c + 1) * P], w1[:, b, :],
                                                start=True, stop=True)
                    last.then_inc(attn_made, 1)
                pe.wait_ge(x1_out, i * C + C)
                for q in range(Q):
                    for c in range(C):
                        nc.tensor.matmul(bank[3][:, q * E:(q + 1) * E], x1[:, c, q * P:(q + 1) * P],
                                         router[:, c, :], start=(c == 0), stop=False)
                    for c in range(C):
                        last = nc.tensor.matmul(bank[3][:, q * E:(q + 1) * E], cond_rep[:, c, q // HALVES, :],
                                                router_t[:, c, :], start=False, stop=(c == C - 1))
                last.then_inc(route_made, 1)
                pe.wait_ge(w_in["sw1"], 16)
                pe.wait_ge(w_in["sw3"], 16)
                for m in range(MS):
                    pair = 4 + 2 * (m % 2)
                    if m >= 2:
                        pe.wait_ge(shared_out, i * MS + m - 1)
                    for w, k in ((sw1_sb, pair), (sw3_sb, pair + 1)):
                        for c in range(C):
                            last = nc.tensor.matmul(bank[k][:, :], w[:, c, m * P:(m + 1) * P], x1[:, c, :],
                                                    start=(c == 0), stop=(c == C - 1))
                    last.then_inc(up_made, 1)
                pe.wait_ge(w_in["rw1"], 16)
                pe.wait_ge(s_out, i + 1)
                for e in range(E):
                    if e >= 4:
                        pe.wait_ge(gelu_out, i * E + e - 3)
                    for c in range(C):
                        last = nc.tensor.matmul(bank[e % 4][:, :], rw1_sb[:, e, c, :], x1[:, c, :],
                                                start=(c == 0), stop=(c == C - 1))
                    last.then_inc(hid_made, 1)
                pe.wait_ge(w_in["sw2"], 16)
                pe.wait_ge(w_in["rw2"], 16)
                pe.wait_ge(shared_out, i * MS + MS)
                for c in range(C):
                    cols = slice(c * P, (c + 1) * P)
                    for m in range(MS):
                        nc.tensor.matmul(bank[4 + c][:, :], sw2_sb[:, m, cols], shared[:, m, :],
                                         start=(m == 0), stop=False)
                    for e in range(E):
                        if c == 0:
                            pe.wait_ge(expert_out, i * E + e + 1)
                        last = nc.tensor.matmul(bank[4 + c][:, :], rw2_sb[:, e, cols], expert[:, e, :],
                                                start=False, stop=(e == E - 1))
                    last.then_inc(moe_made, 1)
                pe.wait_ge(w_in["we"], 16)
                pe.wait_ge(x2_out, i * C + C)
                for c in range(C):
                    for k in range(C):
                        last = nc.tensor.matmul(bank[6 + c][:, :], we_sb[:, k, c * P:(c + 1) * P], x2[:, k, :],
                                                start=(k == 0), stop=(k == C - 1))
                    last.then_inc(lin_made, 1)
                pe.wait_ge(w_in["wx"], 16)
                pe.wait_ge(x3_out, i * (C * B) + C * B)
                for n in range(NXZ):
                    q, g = n // 2, n % 2
                    if n >= 4:
                        pe.wait_ge(xz_out, i * NXZ + n - 3)
                    for c in range(C):
                        last = nc.tensor.matmul(bank[n % 4][:, :], x3[:, c, q * P:(q + 1) * P],
                                                wx_sb[:, c, g * XZ_COLS:(g + 1) * XZ_COLS],
                                                start=(c == 0), stop=(c == C - 1))
                    last.then_inc(xz_made, 1)
                pe.wait_ge(xz_out, i * NXZ + NXZ)

            wh_v = wh_sb[:, :, :].rearrange("p c (g j m) -> p c g j m", g=4, j=J)
            staged_v = staged[:, :, :, :].rearrange("p n g (j m) -> p n g j m", j=J)
            groups = ((bank[0], GI, GF + 1, z_if, t_if), (bank[1], GC, GC + 1, z_c, t_c),
                      (bank[2], GO, GO + 1, z_o, t_o))
            pe.wait_ge(w_in["wh"], 16)
            with pe.Fori(0, ITERS) as i:
                count = [pe.snap(i * U + u + 1) for u in range(U)]
                both = pe.snap(i * (16 * B) + 16 * B)
                for u in range(U):
                    now, prev, n, k = count[u], (u - 1) % U, u // HU, u % HU
                    if k == 0:
                        pe.wait_ge(staged_in[n], both)
                    for z, g0, g1, _, taken in groups:
                        pe.wait_ge(taken, now)
                        for j in range(J):
                            last = nc.tensor.matmul(
                                z[32 * j:32 * j + B, 0:(g1 - g0) * HC].rearrange("p (g m) -> p g m", m=HC),
                                ident[:, k:k + HU + 1:HU], staged_v[:, n, g0:g1, j, :],
                                start=True, stop=False, skip_group_check=True)
                    if k == HU - 1:
                        last.then_inc(staged_used[n], 1)
                    pe.wait_ge(hid, now)
                    for z, g0, g1, made, _ in groups:
                        for c in range(C):
                            for j in range(J):
                                last = nc.tensor.matmul(
                                    z[32 * j:32 * j + B, 0:(g1 - g0) * HC].rearrange("p (g m) -> p g m", m=HC),
                                    h_ring[:, prev, c, :], wh_v[:, c, g0:g1, j, :],
                                    start=False, stop=(c == C - 1), skip_group_check=True)
                        last.then_inc(made, 1)


_INS = ("x", "small", "wkv", "wq", "wproj", "sw1", "sw3", "sw2", "rw1", "rw2", "wu", "we", "wproj2", "wx",
        "wh", "bias_z")


def kernel(**inputs):
    import numpy as np
    import concourse.bacc as bacc
    from concourse.bass_utils import run_bass_kernel_spmd

    a = {k: np.asarray(v) for k, v in inputs.items()}

    def fold_rows(w):
        n = w.shape[1]
        return w.reshape(4, 2, 32, n).transpose(0, 2, 1, 3).reshape(P, C, n)

    def fold_cols(w):
        n = w.shape[0]
        return w.reshape(n, 4, 2, 32).transpose(0, 2, 1, 3).reshape(n, D)

    def plain_rows(w):
        return w.reshape(-1, P, w.shape[1]).transpose(1, 0, 2)

    def vector(v):
        return plain_rows(v.reshape(-1, 1))[:, :, 0]

    f = np.float32
    heads = (np.arange(D)[:, None] // (D // HEADS) == np.arange(HEADS)[None, :]).astype(f)
    before = (np.arange(E)[None, :] < np.arange(E)[:, None]).astype(f).reshape(1, E * E)
    parts = {
        "cond": fold_rows(a["cond_1024"].T),
        "b_q": vector(a["L0_cond_b_q"]),
        "b_kv": vector(a["L0_cond_b_kv"]),
        "no_k": vector(a["L0_cond_no_op_k"].reshape(-1)),
        "no_v": vector(a["L0_cond_no_op_v"].reshape(-1)),
        "b_proj": fold_rows(a["L0_cond_b_proj"].reshape(D, 1)),
        "b_proj2": vector(a["L2_cond_b_proj"]),
        "router": fold_rows(a["L1_cond_router_w"].T),
        "router_t": fold_rows(a["L1_cond_router_t_w"].T),
        "router_bias": np.broadcast_to(a["L1_cond_router_bias"][None, :], (P, E)),
        "head": plain_rows(heads),
        "before": np.broadcast_to(before, (P, E * E)),
        "ident": np.eye(P, 16, dtype=f),
    }
    arrays = {
        "x": a["x"].reshape(B, T, 4, 2, 32).transpose(2, 4, 3, 0, 1).reshape(P, C, B, T),
        "small": np.concatenate([parts[n].reshape(P, -1) for n in SMALL], axis=1),
        "wkv": fold_rows(a["L0_cond_W_kv"]),
        "wq": plain_rows(fold_cols(a["L0_cond_W_q"].T)),
        "wproj": plain_rows(fold_cols(a["L0_cond_W_proj"])),
        "sw1": fold_rows(a["L1_cond_sw1"].T),
        "sw3": fold_rows(a["L1_cond_sw3"].T),
        "sw2": plain_rows(fold_cols(a["L1_cond_sw2"].T)),
        "rw1": a["L1_cond_rw1"].reshape(E, P, 4, 2, 32).transpose(2, 4, 0, 3, 1).reshape(P, E, C, P),
        "rw2": np.stack([fold_cols(w.T) for w in a["L1_cond_rw2"]], axis=1),
        "wu": plain_rows(fold_cols(a["L2_cond_weight_matrix"][:D])),
        "we": fold_rows(fold_cols(a["L2_cond_weight_matrix"][D:])),
        "wproj2": fold_rows(a["L2_cond_W_proj"]),
        "wx": fold_rows(a["L3_cond_Wx"]),
        "wh": fold_rows(a["L3_cond_Wh"]),
        "bias_z": np.broadcast_to(a["L3_cond_b"][None, :], (P, G4)),
    }
    nc = bacc.Bacc("TRN2", target_bir_lowering=False, num_devices=1)
    feed, args = {}, []
    for name in _INS:
        v = np.ascontiguousarray(arrays[name])
        feed[f"in_{name}"] = v
        args.append(nc.dram_tensor(f"in_{name}", v.shape, mybir.dt.from_np(v.dtype), kind="ExternalInput").ap())
    args.append(nc.dram_tensor("out_y", (P, C, B, T), F32, kind="ExternalOutput").ap())
    cond_stack_kernel(nc, *args)
    r = run_bass_kernel_spmd(nc, [feed], core_ids=[0])
    y = r.results[0]["out_y"]
    return np.ascontiguousarray(
        y.reshape(4, 32, C, B, T).transpose(3, 4, 0, 2, 1).reshape(B, T, D))
```

```python
from contextlib import ExitStack

import concourse.bass as bass
from concourse import mybir

F32 = mybir.dt.float32
ALU = mybir.AluOpType
ACT = mybir.ActivationFunctionType
AX = mybir.AxisListType

P = 128
B, T, D = 2, 1024, 256
C = D // P
HEADS = 16
HS = 512
MS = HS // P
E = 8
G4 = 4 * D
TOP_K = 2
EPS = 1e-9

CT = 256
CHUNKS = T // CT
NT = B * CT
Q = NT // P
HALVES = CT // P
XZ_COLS = 512
NXZ = Q * (G4 // XZ_COLS)

Q_ORDER = tuple(range(0, Q, HALVES)) + tuple(q for q in range(Q) if q % HALVES)
LIN_BANKS = (4, 7)

U = 8
ITERS = T // U
HU = U // 2
J = 4
HC = D // J
GI, GF, GO, GC = 0, 1, 2, 3
CITERS = CT // U
STORES = 2

UPS = 2 * MS + E
UNITS = MS + E
OUTS = UNITS // 2
JOBS = UPS + C * OUTS
GATE_ITERS = 2
REST_ITERS = CITERS - JOBS - GATE_ITERS
DOWN = 2 * UPS
assert HU == Q and C == 2 and REST_ITERS > 0

SMALL = {}


def _pack_small():
    at = 0
    for name, width in (("cond", C * B), ("b_q", C), ("b_kv", 2 * C), ("no_k", C), ("no_v", C),
                        ("b_proj", C), ("b_proj2", C), ("router", C * E), ("router_t", C * E),
                        ("router_bias", E), ("head", C * HEADS), ("before", E * E), ("ident", 16)):
        SMALL[name] = (at, at + width)
        at += width
    return at


N_SMALL = _pack_small()


def cond_stack_kernel(nc, x, small, wkv, wq, wproj, moe, wu, we, wproj2, wx, wh, bias_z, y):
    ctx = ExitStack()
    with ctx:
        def sb(name, shape):
            return ctx.enter_context(nc.sbuf_tensor(name, shape, F32))

        def sem(name):
            return ctx.enter_context(nc.semaphore(name))

        xz_dram = nc.dram_tensor("xz_scratch", (B, T, G4), F32).ap()
        comb_dram = nc.dram_tensor("comb_scratch", (CHUNKS, NT * E), F32).ap()

        small_sb = sb("small_sb", [P, N_SMALL])
        wkv_sb = sb("wkv_sb", [P, C, 2 * D])
        wq_sb = sb("wq_sb", [P, C, D])
        wproj_sb = sb("wproj_sb", [P, C, D])
        moe_sb = sb("moe_sb", [P, 2 * JOBS, P])
        wu_sb = sb("wu_sb", [P, C, D])
        we_sb = sb("we_sb", [P, C, D])
        wproj2_sb = sb("wproj2_sb", [P, C, D])
        wx_sb = sb("wx_sb", [P, C, G4])
        wh_sb = sb("wh_sb", [P, C, G4])
        bias_z_sb = sb("bias_z_sb", [P, G4])

        def part(name, pattern=None, **kw):
            ap = small_sb[:, SMALL[name][0]:SMALL[name][1]]
            return ap.rearrange(pattern, **kw) if pattern else ap

        cond = part("cond", "p (c b) -> p c b", c=C)
        b_q = part("b_q")
        b_kv = part("b_kv")
        no_k, no_v = part("no_k"), part("no_v")
        b_proj, b_proj2 = part("b_proj"), part("b_proj2")
        router = part("router", "p (c e) -> p c e", c=C)
        router_t = part("router_t", "p (c e) -> p c e", c=C)
        router_bias = part("router_bias")
        head = part("head", "p (c h) -> p c h", c=C)
        before = part("before", "p (e f) -> p e f", e=E)
        ident = part("ident")

        stream = sb("stream", [P, C, B, T])

        kv = sb("kv", [P, 2 * C, B])
        k_diff = sb("k_diff", [P, C, B])
        v_diff = sb("v_diff", [P, C, B])
        k_heads = sb("k_heads", [P, C, B, HEADS])
        v_heads = sb("v_heads", [P, C, B, HEADS])
        score_w = sb("score_w", [P, C, B, HEADS])
        score_b = sb("score_b", [HEADS, B])
        value_w = sb("value_w", [HEADS, B, D])
        attn_b = sb("attn_b", [P, C])
        cond_rep = sb("cond_rep", [P, C, B, P])
        u_act = sb("u_act", [P, C, B])
        cond_out = sb("cond_out", [P, C, B])

        w1 = sb("w1", [HEADS, B, CT])
        x1 = sb("x1", [P, C, NT])
        x2 = sb("x2", [P, C, NT])
        x3 = sb("x3", [P, C, NT])
        s_all = sb("s_all", [P, Q, E])
        sel = sb("sel", [P, Q, E])
        beats = sb("beats", [P, Q, E, E])
        ties = sb("ties", [P, Q, E, E])
        rank = sb("rank", [P, Q, E])
        s_top = sb("s_top", [P, Q, E])
        top = sb("top", [P, Q, E])
        den = sb("den", [P, Q])
        den_eps = sb("den_eps", [P, Q])
        den_inv = sb("den_inv", [P, Q])
        den_ok = sb("den_ok", [P, Q])
        inv_ok = sb("inv_ok", [P, Q])
        half_bad = sb("half_bad", [P, Q])
        comb_a = sb("comb_a", [P, Q, E])
        comb_b = sb("comb_b", [P, Q, E])
        comb = sb("comb", [P, Q, E])
        comb_all = sb("comb_all", [P, NT, E])
        sig = sb("sig", [P, 2, NT])
        gated = sb("gated", [P, 2, NT])
        gate_in = sb("gate_in", [P, NT])
        hidden = sb("hidden", [P, UNITS, NT])
        xz_sb = sb("xz_sb", [P, Q, G4])

        staged = sb("staged", [P, 2, 4, D])
        blocks = sb("blocks", [P, 2, P])
        h_ring = sb("h_ring", [P, U, C, B])
        if_act = sb("if_act", [P, 2, 2, C * B, 2])
        o_act = sb("o_act", [P, 2, C * B])

        bank = [ctx.enter_context(nc.psum_tensor(f"bank{n}", [P, 512], F32)) for n in range(8)]

        t_if_b = bank[3][:, 0:3 * HC].rearrange("p (g c r) -> p g c r", g=3, r=32)
        t_c_b = bank[4][:, 0:HC].rearrange("p (c r) -> p c r", r=32)
        cell_b = bank[5][:, 0:4 * C * B].rearrange("p (v q k) -> p v q k", v=2, k=2)
        g_pairs = bank[6][:, 0:4 * C * B].rearrange("p (v q k) -> p v q k", v=2, k=2)
        c_tanh = bank[6][:, 4 * C * B:6 * C * B].rearrange("p (v q) -> p v q", v=2)

        small_in = sem("small_in")
        x_in = sem("x_in")
        w_in = {n: sem(f"{n}_in") for n in ("wkv", "wq", "wproj", "up", "down", "wu", "we", "wproj2",
                                            "wx", "wh", "bias_z")}
        kv_made = sem("kv_made")
        kv_out = sem("kv_out")
        diff_made = sem("diff_made")
        heads_made = sem("heads_made")
        u_made = sem("u_made")
        u_out = sem("u_out")
        setup_made = sem("setup_made")
        setup_out = sem("setup_out")
        rep_made = sem("rep_made")
        d_made = sem("d_made")
        w1_out = sem("w1_out")
        attn_made = sem("attn_made")
        x1_out = sem("x1_out")
        x1_kept = sem("x1_kept")
        route_made = sem("route_made")
        s_out = sem("s_out")
        top_step = sem("top_step")
        comb_out = sem("comb_out")
        comb_stored = sem("comb_stored")
        comb_in = sem("comb_in")
        up_made = sem("up_made")
        sig_out = sem("sig_out")
        gated_out = sem("gated_out")
        shared_out = sem("shared_out")
        hid_made = sem("hid_made")
        gelu_out = sem("gelu_out")
        expert_out = sem("expert_out")
        moe_made = sem("moe_made")
        x2_out = sem("x2_out")
        lin_made = sem("lin_made")
        x3_out = sem("x3_out")
        x3_kept = sem("x3_kept")
        xz_made = sem("xz_made")
        xz_out = sem("xz_out")
        xz_stored = [sem(f"xz_stored{q}") for q in range(Q)]
        z_if = sem("z_if")
        z_c = sem("z_c")
        z_o = sem("z_o")
        t_if = sem("t_if")
        t_c = sem("t_c")
        t_o = sem("t_o")
        a_if = sem("a_if")
        a_c = sem("a_c")
        a_o = sem("a_o")
        kept = sem("kept")
        cell = sem("cell")
        cell_tanh = sem("cell_tanh")
        hid = sem("hid")
        staged_clear = sem("staged_clear")
        staged_in = [sem(f"staged_in{n}") for n in range(2)]
        staged_used = [sem(f"staged_used{n}") for n in range(2)]
        added = sem("added")
        block_in = [sem(f"block_in{n}") for n in range(2)]
        block_used = [sem(f"block_used{n}") for n in range(2)]
        job_taken = sem("job_taken")
        side_sig = sem("side_sig")
        side_gated = sem("side_gated")
        side_gelu = sem("side_gelu")
        y_stored = sem("y_stored")

        block = ctx.enter_context(nc.Block())

        @block.sync
        def _(sp):
            sp.dma_start(small_sb[:, :], small).then_inc(small_in, 16)
            for name, dst, src in (("wkv", wkv_sb, wkv), ("wq", wq_sb, wq), ("wproj", wproj_sb, wproj),
                                   ("up", moe_sb[:, 0:DOWN, :], moe[:, 0:DOWN, :]),
                                   ("down", moe_sb[:, DOWN:, :], moe[:, DOWN:, :]), ("we", we_sb, we),
                                   ("wx", wx_sb, wx), ("bias_z", bias_z_sb, bias_z), ("wh", wh_sb, wh)):
                sp.dma_start(dst[:], src).then_inc(w_in[name], 16)

            with sp.Fori(0, CHUNKS) as i:
                sp.wait_ge(comb_out, i + 1)
                sp.dma_start(comb_dram[bass.ds(i, 1), :].rearrange("a (q p e) -> p (a q) e", q=Q, e=E),
                             comb[:, :, :]).then_inc(comb_stored, 16)
            sp.wait_ge(comb_stored, 16 * (CHUNKS + 1))

            def spread(m):
                sp.dma_start(comb_all[:, :, :].rearrange("p n e -> p (n e)"),
                             comb_dram[bass.ds(m, 1), :].partition_broadcast(P).rearrange("p a n -> p (a n)")
                             ).then_inc(comb_in, 16)

            def gate_inputs(m):
                rows = [sp.snap(m * CT + half * P) for half in range(HALVES)]
                tiles = [sp.snap(m * NXZ + 2 * (at + 1)) for at in range(Q)]
                for at, q in enumerate(Q_ORDER):
                    b, half = q // HALVES, q % HALVES
                    sp.wait_ge(xz_out, tiles[at])
                    if half == 0:
                        for n in range(2):
                            sp.dma_start(staged[b * HU:(b + 1) * HU, n, :, :].rearrange("p g d -> p (g d)"),
                                         xz_sb[n * HU:(n + 1) * HU, q, :]).then_inc(staged_in[n], 16)
                    sp.dma_start(xz_dram[b, bass.ds(rows[half], P), :],
                                 xz_sb[:, q, :]).then_inc(xz_stored[q], 16)

            def gate_inputs_stored(m):
                stored = sp.snap(m * 16 + 32)
                for q in range(Q):
                    sp.wait_ge(xz_stored[q], stored)

            def stage(used, n, at):
                sp.wait_ge(staged_used[n], used)
                for b in range(B):
                    sp.dma_start(staged[b * HU:(b + 1) * HU, n, :, :].rearrange("p g d -> p (g d)"),
                                 xz_dram[b, bass.ds(at, HU), :]).then_inc(staged_in[n], 16)

            def bring(used, n, block_):
                sp.wait_ge(block_used[n], used)
                sp.dma_start(blocks[:, n, :], moe_sb[:, bass.ds(block_, 1), :].rearrange("p a n -> p (a n)")
                             ).then_inc(block_in[n], 16)

            def rounds(i, first, length, job=None):
                with sp.Fori(0, length) as k:
                    at = [sp.snap(i * CT + k * U + (first * U + U + n * HU)) for n in range(2)]
                    used = sp.snap(i * CITERS + k + (first + 1))
                    if job is not None:
                        jobs = sp.snap(i * JOBS + k + (job + 1))
                        block_ = [sp.snap(k * 2 + (2 * job + n)) for n in range(2)]
                    for n in range(2):
                        stage(used, n, at[n])
                        if job is not None:
                            bring(jobs, n, block_[n])

            per_store = CITERS // STORES

            def store(i, piece):
                at, count = sp.snap(i * CT + piece * per_store * U), sp.snap(
                    i * CITERS + ((piece + 1) * per_store + 1))
                sp.wait_ge(added, count)
                sp.dma_start(y[:, :, :, bass.ds(at, per_store * U)],
                             stream[:, :, :, bass.ds(at, per_store * U)]).then_inc(y_stored, 16)

            spread(0)
            sp.wait_ge(w_in["up"], 16)
            for n in range(2):
                bring(1, n, n)
            sp.wait_ge(staged_clear, 1)
            gate_inputs(0)
            with sp.Fori(0, CHUNKS - 1) as i:
                chunk_, scaled = sp.snap(i + 1), sp.snap(i * E + E)
                gate_inputs_stored(i)
                sp.wait_ge(w_in["down"], 16)
                sp.wait_ge(expert_out, scaled)
                spread(chunk_)
                assert per_store == UPS
                rounds(i, 0, UPS, 1)
                store(i, 0)
                rounds(i, UPS, GATE_ITERS)
                rounds(i, UPS + GATE_ITERS, C * OUTS - 1, UPS + 1)
                jobs = sp.snap(i * JOBS + (JOBS + 1))
                for n in range(2):
                    bring(jobs, n, n)
                rounds(i, CITERS - REST_ITERS - 1, REST_ITERS)
                store(i, 1)
                used = sp.snap(i * CITERS + CITERS)
                for n in range(2):
                    sp.wait_ge(staged_used[n], used)
                gate_inputs(i + 1)
            gate_inputs_stored(CHUNKS - 1)
            for piece in range(STORES):
                rounds(CHUNKS - 1, piece * per_store, per_store - piece)
                store(CHUNKS - 1, piece)
            sp.wait_ge(y_stored, 16 * STORES * CHUNKS)

        @block.gpsimd
        def _(pool):
            pool.sem_inc(x3_kept, 1)
            for q in range(Q):
                pool.sem_inc(xz_stored[q], 16)
            pool.sem_inc(added, 1)
            pool.sem_inc(comb_stored, 16)
            pool.sem_inc(x1_kept, 1)
            for n in range(2):
                pool.sem_inc(block_used[n], 1)
            pool.sem_inc(job_taken, 1)
            pool.memset(staged[:, :, :, :], 0.0).then_inc(staged_clear, 1)
            with pool.Fori(0, CHUNKS) as i:
                pool.wait_ge(x1_out, i * C + C)
                pool.tensor_copy(stream[:, :, :, bass.ds(i * CT, CT)],
                                 x1[:, :, :].rearrange("p c (b t) -> p c b t", b=B)).then_inc(x1_kept, 1)

            def keep(m):
                pool.wait_ge(x3_out, m * (C * B) + C * B)
                pool.tensor_copy(stream[:, :, :, bass.ds(m * CT, CT)],
                                 x3[:, :, :].rearrange("p c (b t) -> p c b t", b=B)).then_inc(x3_kept, 1)

            def add(m, it):
                pool.wait_ge(x3_kept, m + 2)
                pool.wait_ge(hid, it * U + U + 1)
                out = stream[:, :, :, bass.ds(it * U, U)].rearrange("p c b t -> p (c b) t")
                pool.tensor_tensor(out, out, h_ring[:, :, :, :].rearrange("p u c b -> p (c b) u"),
                                   ALU.add).then_inc(added, 1)

            keep(0)
            with pool.Fori(0, CHUNKS - 1) as i:
                with pool.Fori(0, CITERS) as k:
                    add(i, i * CITERS + k)
                keep(i + 1)
            with pool.Fori(0, CITERS) as k:
                add(CHUNKS - 1, k + (CHUNKS - 1) * CITERS)

        @block.scalar
        def _(act):
            act.dma_start(wproj2_sb[:], wproj2).then_inc(w_in["wproj2"], 16)
            act.dma_start(wu_sb[:], wu).then_inc(w_in["wu"], 16)
            act.dma_start(stream[:, :, :, :], x).then_inc(x_in, 16)
            act.wait_ge(small_in, 16)
            act.wait_ge(u_made, 1)
            for m in range(C):
                nc.scalar.activation(u_act[:, m, :], bank[4][:, m * B:(m + 1) * B], ACT.Gelu,
                                     bias=b_proj2[:, m:m + 1]).then_inc(u_out, 1)
            act.wait_ge(setup_out, 5)
            with act.Fori(0, CHUNKS) as i:
                act.wait_ge(d_made, i + 1)
                for b in range(B):
                    nc.scalar.activation(w1[:, b, :], bank[0][0:HEADS, b * CT:(b + 1) * CT], ACT.Sigmoid,
                                         bias=score_b[:, b:b + 1]).then_inc(w1_out, 1)
                act.wait_ge(route_made, i + 1)
                nc.scalar.activation(s_all[:, :, :].rearrange("p q e -> p (q e)"), bank[3][:, 0:Q * E],
                                     ACT.Sigmoid).then_inc(s_out, 1)
            for m in range(MS):
                act.wait_ge(up_made, m + 1)
                if m >= 2:
                    act.wait_ge(gated_out, m - 1)
                nc.scalar.activation(sig[:, m % 2, :], bank[4 + 2 * (m % 2)][:, :],
                                     ACT.Sigmoid).then_inc(sig_out, 1)
            for e in range(E):
                act.wait_ge(hid_made, e + 1)
                nc.scalar.activation(hidden[:, MS + e, :], bank[e % 4][:, :], ACT.Gelu).then_inc(gelu_out, 1)

            def steps(it, side=None):
                begun = [act.snap(it * U + u + 2) for u in range(U)]
                for u in range(U):
                    if side and u in side:
                        side[u]()
                    par, now = u % 2, begun[u]
                    act.wait_ge(t_if, now)
                    nc.scalar.activation(if_act[:, par, :, :, 0], t_if_b[:, 0:2, :, 0:B],
                                         ACT.Sigmoid).then_inc(a_if, 1)
                    act.wait_ge(t_c, now)
                    nc.scalar.activation(g_pairs[:, par, :, 1], t_c_b[:, :, 0:B], ACT.Tanh).then_inc(a_c, 1)
                    act.wait_ge(t_o, now)
                    nc.scalar.activation(o_act[:, par, :], t_if_b[:, 2, :, 0:B], ACT.Sigmoid).then_inc(a_o, 1)
                    act.wait_ge(cell, now)
                    nc.scalar.activation(c_tanh[:, par, :], cell_b[:, par, :, 1],
                                         ACT.Tanh).then_inc(cell_tanh, 1)

            act.preload_act_table_set("sigmoid_and_others")
            with act.Fori(0, CHUNKS - 1) as i:
                with act.Fori(0, MS) as m:
                    def side_sigmoid():
                        act.wait_ge(job_taken, i * UPS + m * 2 + 2)
                        nc.scalar.activation(sig[:, 0, :], gate_in[:, :], ACT.Sigmoid).then_inc(side_sig, 1)

                    steps(i * CITERS + m * 2)
                    steps(i * CITERS + m * 2 + 1, {0: side_sigmoid})
                with act.Fori(0, E) as k:
                    steps(i * CITERS + k + 2 * MS)

                def side_gelus():
                    act.wait_ge(job_taken, i * UPS + UPS + 1)
                    nc.scalar.activation(hidden[:, MS:UNITS, :], hidden[:, MS:UNITS, :],
                                         ACT.Gelu).then_inc(side_gelu, 1)
                    act.preload_act_table_set("sigmoid_and_others")

                steps(i * CITERS + UPS, {0: side_gelus})
                with act.Fori(0, CITERS - UPS - 1) as k:
                    steps(i * CITERS + k + (UPS + 1))
            with act.Fori(0, CITERS) as k:
                steps(k + (CHUNKS - 1) * CITERS)

        @block.vector
        def _(dve):
            def pairs(ap):
                return ap.unsqueeze(2).to_broadcast([P, C, B])

            dve.wait_ge(small_in, 16)
            nc.vector.tensor_copy(cond_rep[:, :, :, :],
                                  cond.unsqueeze(3).to_broadcast([P, C, B, P])).then_inc(rep_made, 1)
            dve.wait_ge(kv_made, 1)
            nc.vector.tensor_tensor(kv[:, :, :], bank[0][:, 0:2 * C * B].rearrange("p (m b) -> p m b", b=B),
                                    b_kv.unsqueeze(2).to_broadcast([P, 2 * C, B]), ALU.add).then_inc(kv_out, 1)
            dve.wait_ge(kv_out, 1)
            nc.vector.tensor_tensor(k_diff[:, :, :], kv[:, 0:C, :], pairs(no_k), ALU.subtract).then_inc(diff_made, 1)
            nc.vector.tensor_tensor(v_diff[:, :, :], kv[:, C:2 * C, :], pairs(no_v),
                                    ALU.subtract).then_inc(diff_made, 1)
            dve.wait_ge(diff_made, 2)
            for dst, src in ((k_heads, k_diff), (v_heads, v_diff)):
                for m in range(C):
                    nc.vector.tensor_tensor(dst[:, m, :, :],
                                            head[:, m, :].unsqueeze(1).to_broadcast([P, B, HEADS]),
                                            src[:, m, :].unsqueeze(2).to_broadcast([P, B, HEADS]),
                                            ALU.mult).then_inc(heads_made, 1)
            dve.wait_ge(setup_made, 1)
            nc.vector.tensor_copy(score_w[:, :, :, :].rearrange("p c b h -> p (c b h)"),
                                  bank[1][:, 0:C * B * HEADS]).then_inc(setup_out, 1)
            dve.wait_ge(setup_made, 2)
            nc.vector.tensor_copy(score_b[:, :], bank[2][0:HEADS, 0:B]).then_inc(setup_out, 1)
            nc.vector.tensor_tensor(attn_b[:, :], bank[2][:, 8:8 + C], b_proj, ALU.add).then_inc(setup_out, 1)
            dve.wait_ge(setup_made, 3)
            nc.vector.tensor_copy(value_w[:, :, :].rearrange("h b d -> h (b d)"),
                                  bank[3][0:HEADS, :]).then_inc(setup_out, 1)
            dve.wait_ge(setup_made, 4)
            nc.vector.tensor_copy(cond_out[:, :, :].rearrange("p c b -> p (c b)"),
                                  bank[5][:, 0:C * B]).then_inc(setup_out, 1)
            dve.wait_ge(setup_out, 5)
            dve.wait_ge(x_in, 16)

            with dve.Fori(0, CHUNKS) as i:
                dve.wait_ge(x1_kept, i + 1)
                for c in range(C):
                    dve.wait_ge(attn_made, i * C + c + 1)
                    nc.vector.scalar_tensor_tensor(
                        out=x1[:, c, :].rearrange("p (b t) -> p b t", b=B),
                        in0=bank[1 + c][:, :].rearrange("p (b t) -> p b t", b=B), scalar=attn_b[:, c:c + 1],
                        in1=stream[:, c, :, bass.ds(i * CT, CT)], op0=ALU.add, op1=ALU.add).then_inc(x1_out, 1)

                steps = 11
                done = [0]

                def step(ins):
                    done[0] += 1
                    ins.then_inc(top_step, 1)
                    dve.wait_ge(top_step, i * steps + done[0])

                rivals = sel[:, :, :].unsqueeze(2).to_broadcast([P, Q, E, E])
                own = sel[:, :, :].unsqueeze(3).to_broadcast([P, Q, E, E])
                dve.wait_ge(s_out, i + 1)
                step(nc.vector.tensor_tensor(sel[:, :, :], s_all[:, :, :],
                                             router_bias.unsqueeze(1).to_broadcast([P, Q, E]), ALU.add))
                nc.vector.tensor_tensor(beats[:, :, :, :], rivals, own, ALU.is_gt)
                step(nc.vector.tensor_tensor(ties[:, :, :, :], rivals, own, ALU.is_equal))
                step(nc.vector.tensor_tensor(ties[:, :, :, :], ties[:, :, :, :],
                                             before.unsqueeze(1).to_broadcast([P, Q, E, E]), ALU.mult))
                step(nc.vector.tensor_tensor(beats[:, :, :, :], beats[:, :, :, :], ties[:, :, :, :], ALU.add))
                step(nc.vector.tensor_reduce(rank[:, :, :], beats[:, :, :, :], AX.X, ALU.add))
                nc.vector.tensor_scalar(top[:, :, :], rank[:, :, :], float(TOP_K), None, ALU.is_lt)
                step(nc.vector.scalar_tensor_tensor(out=s_top[:, :, :], in0=rank[:, :, :], scalar=float(TOP_K),
                                                    in1=s_all[:, :, :], op0=ALU.is_lt, op1=ALU.mult))
                step(nc.vector.tensor_reduce(den[:, :], s_top[:, :, :], AX.X, ALU.add))
                nc.vector.tensor_scalar(den_ok[:, :], den[:, :], EPS, None, ALU.is_gt)
                step(nc.vector.tensor_scalar(den_eps[:, :], den[:, :], EPS, None, ALU.add))
                nc.vector.tensor_scalar(half_bad[:, :], den_ok[:, :], -1.0 / TOP_K, 1.0 / TOP_K, ALU.mult, ALU.add)
                step(nc.vector.reciprocal(den_inv[:, :], den_eps[:, :]))
                nc.vector.tensor_tensor(comb_b[:, :, :], top[:, :, :],
                                        half_bad[:, :].unsqueeze(2).to_broadcast([P, Q, E]), ALU.mult)
                step(nc.vector.tensor_tensor(inv_ok[:, :], den_inv[:, :], den_ok[:, :], ALU.mult))
                step(nc.vector.tensor_tensor(comb_a[:, :, :], s_top[:, :, :],
                                             inv_ok[:, :].unsqueeze(2).to_broadcast([P, Q, E]), ALU.mult))
                dve.wait_ge(comb_stored, i * 16 + 16)
                nc.vector.tensor_tensor(comb[:, :, :], comb_a[:, :, :], comb_b[:, :, :],
                                        ALU.add).then_inc(comb_out, 1)
                assert done[0] == steps

            for m in range(MS):
                pair = 4 + 2 * (m % 2)
                dve.wait_ge(sig_out, m + 1)
                nc.vector.tensor_tensor(gated[:, m % 2, :], sig[:, m % 2, :], bank[pair][:, :],
                                        ALU.mult).then_inc(gated_out, 1)
                dve.wait_ge(gated_out, m + 1)
                nc.vector.tensor_tensor(hidden[:, m, :], gated[:, m % 2, :], bank[pair + 1][:, :],
                                        ALU.mult).then_inc(shared_out, 1)

            def scale(e):
                nc.vector.tensor_tensor(hidden[:, MS + e, :], hidden[:, MS + e, :], comb_all[:, :, e],
                                        ALU.mult).then_inc(expert_out, 1)

            def layer2(m, c, src):
                nc.vector.scalar_tensor_tensor(out=x2[:, c, :].rearrange("p (b t) -> p b t", b=B),
                                               in0=src[:, :].rearrange("p (b t) -> p b t", b=B),
                                               scalar=1.0 / (1 + TOP_K),
                                               in1=stream[:, c, :, bass.ds(m * CT, CT)], op0=ALU.mult,
                                               op1=ALU.add).then_inc(x2_out, 1)

            def finish(m):
                dve.wait_ge(x3_kept, m + 1)
                for c in range(C):
                    dve.wait_ge(lin_made, m * C + c + 1)
                    for b in range(B):
                        cols = slice(b * CT, (b + 1) * CT)
                        nc.vector.scalar_tensor_tensor(out=x3[:, c, cols], in0=bank[LIN_BANKS[c]][:, cols],
                                                       scalar=cond_out[:, c, b:b + 1], in1=x2[:, c, cols],
                                                       op0=ALU.add, op1=ALU.add).then_inc(x3_out, 1)
                for n in range(NXZ):
                    q, g = Q_ORDER[n // 2], n % 2
                    cols = slice(g * XZ_COLS, (g + 1) * XZ_COLS)
                    if g == 0:
                        dve.wait_ge(xz_stored[q], m * 16 + 16)
                    dve.wait_ge(xz_made, m * NXZ + n + 1)
                    nc.vector.tensor_tensor(xz_sb[:, q, cols], bank[n % 4][:, :], bias_z_sb[:, cols],
                                            ALU.add).then_inc(xz_out, 1)

            dve.wait_ge(comb_in, 16)
            for e in range(E):
                dve.wait_ge(gelu_out, e + 1)
                scale(e)
            dve.wait_ge(x1_kept, CHUNKS + 1)
            for c in range(C):
                dve.wait_ge(moe_made, c + 1)
                layer2(0, c, bank[4 + c])
            dve.wait_ge(w_in["bias_z"], 16)
            finish(0)

            dve.wait_ge(xz_out, NXZ)
            nc.vector.memset(bank[0][:, :], 0.0).then_inc(t_if, 1)
            nc.vector.memset(bank[1][:, :], 0.0).then_inc(t_c, 1)
            nc.vector.memset(bank[2][:, :], 0.0).then_inc(t_o, 1)
            nc.vector.memset(bank[6][:, 0:6 * C * B], 0.0)
            nc.vector.memset(bank[5][:, 0:4 * C * B], 0.0).then_inc(cell, 1)
            nc.vector.tensor_copy(h_ring[:, U - 1, :, :], cond).then_inc(hid, 1)

            def steps(it, side=None):
                added_count = dve.snap(it + 1)
                count = [dve.snap(it * U + u + 1) for u in range(U)]
                for u in range(U):
                    if side and u in side:
                        side[u]()
                    par, now = u % 2, count[u]
                    dve.wait_ge(z_if, now)
                    nc.vector.transpose(bank[3][:, 0:2 * HC], bank[0][:, 0:2 * HC]).then_inc(t_if, 1)
                    dve.wait_ge(z_c, now)
                    nc.vector.transpose(bank[4][:, 0:HC], bank[1][:, 0:HC]).then_inc(t_c, 1)
                    dve.wait_ge(a_if, now)
                    dve.wait_ge(cell, now)
                    nc.vector.tensor_tensor(if_act[:, par, 0, :, 1], if_act[:, par, 1, :, 0],
                                            cell_b[:, 1 - par, :, 1], ALU.mult).then_inc(kept, 1)
                    dve.wait_ge(z_o, now)
                    nc.vector.transpose(bank[3][:, 2 * HC:3 * HC], bank[2][:, 0:HC]).then_inc(t_o, 1)
                    dve.wait_ge(a_c, now)
                    dve.wait_ge(kept, now)
                    nc.vector.tensor_tensor_scan(cell_b[:, par, :, :].rearrange("p q k -> p (q k)"),
                                                 g_pairs[:, par, :, :].rearrange("p q k -> p (q k)"),
                                                 if_act[:, par, 0, :, :].rearrange("p q k -> p (q k)"), 0.0,
                                                 ALU.mult, ALU.add).then_inc(cell, 1)
                    dve.wait_ge(cell_tanh, now)
                    dve.wait_ge(a_o, now)
                    if u == 0:
                        dve.wait_ge(added, added_count)
                    nc.vector.tensor_tensor(h_ring[:, u, :, :].rearrange("p c b -> p (c b)"), o_act[:, par, :],
                                            c_tanh[:, par, :], ALU.mult).then_inc(hid, 1)

            def job_made(i, k):
                dve.wait_ge(block_used[1], i * JOBS + k + 2)

            with dve.Fori(0, CHUNKS - 1) as i:
                with dve.Fori(0, MS) as m:
                    def take_gate():
                        job_made(i, m * 2)
                        nc.vector.tensor_copy(gate_in[:, :], bank[7][:, :]).then_inc(job_taken, 1)

                    def side_gate():
                        dve.wait_ge(side_sig, i * MS + m + 1)
                        nc.vector.tensor_tensor(gated[:, 0, :], sig[:, 0, :], gate_in[:, :],
                                                ALU.mult).then_inc(side_gated, 1)

                    def take_shared():
                        job_made(i, m * 2 + 1)
                        dve.wait_ge(side_gated, i * MS + m + 1)
                        nc.vector.tensor_tensor(hidden[:, bass.ds(m, 1), :].rearrange("p a n -> p (a n)"),
                                                gated[:, 0, :], bank[7][:, :], ALU.mult).then_inc(job_taken, 1)

                    steps(i * CITERS + m * 2, {U - 1: take_gate})
                    steps(i * CITERS + m * 2 + 1, {2: side_gate, U - 1: take_shared})
                with dve.Fori(0, E) as e:
                    def take_expert():
                        job_made(i, e + 2 * MS)
                        nc.vector.tensor_copy(hidden[:, bass.ds(e + MS, 1), :].rearrange("p a n -> p (a n)"),
                                              bank[7][:, :]).then_inc(job_taken, 1)

                    steps(i * CITERS + e + 2 * MS, {U - 1: take_expert})

                def side_scale(e):
                    def run():
                        if e == 0:
                            dve.wait_ge(side_gelu, i + 1)
                            dve.wait_ge(comb_in, i * 16 + 32)
                        scale(e)
                    return run

                steps(i * CITERS + UPS, {e + 1: side_scale(e) for e in range(U - 1)})
                steps(i * CITERS + UPS + 1, {e + 1 - U: side_scale(e) for e in range(U - 1, E)})
                for c in range(C):
                    def take_out():
                        job_made(i, UPS + c * OUTS + OUTS - 1)
                        layer2(i + 1, c, bank[7])

                    first = UPS + GATE_ITERS + c * OUTS
                    with dve.Fori(0, OUTS - 1) as k:
                        steps(i * CITERS + k + first)
                    steps(i * CITERS + first + OUTS - 1, {U - 1: take_out})
                with dve.Fori(0, REST_ITERS) as k:
                    steps(i * CITERS + k + (CITERS - REST_ITERS))
                finish(i + 1)
            with dve.Fori(0, CITERS) as k:
                steps(k + (CHUNKS - 1) * CITERS)

        @block.tensor
        def _(pe):
            pe.wait_ge(small_in, 16)
            pe.wait_ge(w_in["wproj2"], 16)
            for m in range(C):
                for c in range(C):
                    last = nc.tensor.matmul(bank[4][:, m * B:(m + 1) * B], wproj2_sb[:, c, m * P:(m + 1) * P],
                                            cond[:, c, :], start=(c == 0), stop=(c == C - 1))
            last.then_inc(u_made, 1)
            pe.wait_ge(w_in["wkv"], 16)
            for m in range(2 * C):
                for c in range(C):
                    last = nc.tensor.matmul(bank[0][:, m * B:(m + 1) * B], wkv_sb[:, c, m * P:(m + 1) * P],
                                            cond[:, c, :], start=(c == 0), stop=(c == C - 1))
            last.then_inc(kv_made, 1)
            pe.wait_ge(w_in["wq"], 16)
            pe.wait_ge(heads_made, 2 * C)
            for c in range(C):
                for m in range(C):
                    last = nc.tensor.matmul(bank[1][:, c * B * HEADS:(c + 1) * B * HEADS],
                                            wq_sb[:, m, c * P:(c + 1) * P],
                                            k_heads[:, m, :, :].rearrange("p b h -> p (b h)"),
                                            start=(m == 0), stop=(m == C - 1))
            last.then_inc(setup_made, 1)
            for b in range(B):
                for m in range(C):
                    nc.tensor.matmul(bank[2][0:HEADS, b:b + 1], k_heads[:, m, b, :], b_q[:, m:m + 1],
                                     start=(m == 0), stop=(m == C - 1))
            pe.wait_ge(w_in["wproj"], 16)
            for c in range(C):
                for m in range(C):
                    last = nc.tensor.matmul(bank[2][:, 8 + c:9 + c], wproj_sb[:, m, c * P:(c + 1) * P],
                                            no_v[:, m:m + 1], start=(m == 0), stop=(m == C - 1))
            last.then_inc(setup_made, 1)
            for b in range(B):
                for m in range(C):
                    last = nc.tensor.matmul(bank[3][0:HEADS, b * D:(b + 1) * D], v_heads[:, m, b, :],
                                            wproj_sb[:, m, :], start=(m == 0), stop=(m == C - 1))
            last.then_inc(setup_made, 1)
            pe.wait_ge(w_in["wu"], 16)
            pe.wait_ge(u_out, C)
            for c in range(C):
                for m in range(C):
                    last = nc.tensor.matmul(bank[5][:, c * B:(c + 1) * B], wu_sb[:, m, c * P:(c + 1) * P],
                                            u_act[:, m, :], start=(m == 0), stop=(m == C - 1))
            last.then_inc(setup_made, 1)
            pe.wait_ge(setup_out, 5)
            pe.wait_ge(rep_made, 1)
            pe.wait_ge(x_in, 16)

            with pe.Fori(0, CHUNKS) as i:
                for b in range(B):
                    for c in range(C):
                        last = nc.tensor.matmul(bank[0][0:HEADS, b * CT:(b + 1) * CT], score_w[:, c, b, :],
                                                stream[:, c, b, bass.ds(i * CT, CT)],
                                                start=(c == 0), stop=(c == C - 1))
                last.then_inc(d_made, 1)
                pe.wait_ge(w1_out, i * B + B)
                for c in range(C):
                    for b in range(B):
                        last = nc.tensor.matmul(bank[1 + c][:, b * CT:(b + 1) * CT],
                                                value_w[:, b, c * P:(c + 1) * P], w1[:, b, :],
                                                start=True, stop=True)
                    last.then_inc(attn_made, 1)
                pe.wait_ge(x1_out, i * C + C)
                for q in range(Q):
                    for c in range(C):
                        nc.tensor.matmul(bank[3][:, q * E:(q + 1) * E], x1[:, c, q * P:(q + 1) * P],
                                         router[:, c, :], start=(c == 0), stop=False)
                    for c in range(C):
                        last = nc.tensor.matmul(bank[3][:, q * E:(q + 1) * E], cond_rep[:, c, q // HALVES, :],
                                                router_t[:, c, :], start=False, stop=(c == C - 1))
                last.then_inc(route_made, 1)
                pe.wait_ge(s_out, i + 1)

            pe.wait_ge(w_in["up"], 16)
            pe.wait_ge(x1_kept, CHUNKS + 1)
            for m in range(MS):
                pair = 4 + 2 * (m % 2)
                if m >= 2:
                    pe.wait_ge(shared_out, m - 1)
                for w in range(2):
                    for c in range(C):
                        last = nc.tensor.matmul(bank[pair + w][:, :].rearrange("p (b t) -> p b t", b=B),
                                                moe_sb[:, 2 * (2 * m + w) + c, :], stream[:, c, :, 0:CT],
                                                start=(c == 0), stop=(c == C - 1))
                last.then_inc(up_made, 1)
            for e in range(E):
                if e >= 4:
                    pe.wait_ge(gelu_out, e - 3)
                for c in range(C):
                    last = nc.tensor.matmul(bank[e % 4][:, :].rearrange("p (b t) -> p b t", b=B),
                                            moe_sb[:, 2 * (2 * MS + e) + c, :], stream[:, c, :, 0:CT],
                                            start=(c == 0), stop=(c == C - 1))
                last.then_inc(hid_made, 1)
            pe.wait_ge(w_in["down"], 16)
            pe.wait_ge(shared_out, MS)
            for c in range(C):
                for k in range(UNITS):
                    if c == 0 and k >= MS:
                        pe.wait_ge(expert_out, k - MS + 1)
                    last = nc.tensor.matmul(bank[4 + c][:, :], moe_sb[:, DOWN + c * UNITS + k, :],
                                            hidden[:, k, :], start=(k == 0), stop=(k == UNITS - 1))
                last.then_inc(moe_made, 1)

            def finish(m):
                pe.wait_ge(x2_out, m * C + C)
                for c in range(C):
                    for k in range(C):
                        last = nc.tensor.matmul(bank[LIN_BANKS[c]][:, :], we_sb[:, k, c * P:(c + 1) * P],
                                                x2[:, k, :], start=(k == 0), stop=(k == C - 1))
                    last.then_inc(lin_made, 1)
                pe.wait_ge(x3_out, m * (C * B) + C * B)
                for n in range(NXZ):
                    q, g = Q_ORDER[n // 2], n % 2
                    if n >= 4:
                        pe.wait_ge(xz_out, m * NXZ + n - 3)
                    for c in range(C):
                        last = nc.tensor.matmul(bank[n % 4][:, :], x3[:, c, q * P:(q + 1) * P],
                                                wx_sb[:, c, g * XZ_COLS:(g + 1) * XZ_COLS],
                                                start=(c == 0), stop=(c == C - 1))
                    last.then_inc(xz_made, 1)

            pe.wait_ge(w_in["we"], 16)
            pe.wait_ge(w_in["wx"], 16)
            finish(0)

            wh_v = wh_sb[:, :, :].rearrange("p c (g j m) -> p c g j m", g=4, j=J)
            staged_v = staged[:, :, :, :].rearrange("p n g (j m) -> p n g j m", j=J)
            groups = ((bank[0], GI, GF + 1, z_if, t_if), (bank[1], GC, GC + 1, z_c, t_c),
                      (bank[2], GO, GO + 1, z_o, t_o))
            pe.wait_ge(w_in["wh"], 16)

            def steps(it, side=None):
                count = [pe.snap(it * U + u + 1) for u in range(U)]
                both = pe.snap(it * (16 * B) + 16 * B)
                for u in range(U):
                    now, prev, n, k = count[u], (u - 1) % U, u // HU, u % HU
                    if k == 0:
                        pe.wait_ge(staged_in[n], both)
                    for z, g0, g1, _, taken in groups:
                        pe.wait_ge(taken, now)
                        for j in range(J):
                            last = nc.tensor.matmul(
                                z[32 * j:32 * j + B, 0:(g1 - g0) * HC].rearrange("p (g m) -> p g m", m=HC),
                                ident[:, k:k + HU + 1:HU], staged_v[:, n, g0:g1, j, :],
                                start=True, stop=False, skip_group_check=True)
                    if k == HU - 1:
                        last.then_inc(staged_used[n], 1)
                    if side:
                        side(u)
                    pe.wait_ge(hid, now)
                    for z, g0, g1, made, _ in groups:
                        for c in range(C):
                            for j in range(J):
                                last = nc.tensor.matmul(
                                    z[32 * j:32 * j + B, 0:(g1 - g0) * HC].rearrange("p (g m) -> p g m", m=HC),
                                    h_ring[:, prev, c, :], wh_v[:, c, g0:g1, j, :],
                                    start=False, stop=(c == C - 1), skip_group_check=True)
                        last.then_inc(made, 1)

            def job(count, u, rhs, start=False, stop=False, free=None):
                n, tile = u // Q, u % Q
                if tile == 0:
                    pe.wait_ge(block_in[n], count * 16 + 16)
                if u == 0 and free:
                    free()
                last = nc.tensor.matmul(bank[7][:, tile * P:(tile + 1) * P], blocks[:, n, :], rhs(n, tile),
                                        start=start and u == 0, stop=stop and n == 1, skip_group_check=True)
                if tile == Q - 1:
                    last.then_inc(block_used[n], 1)

            with pe.Fori(0, CHUNKS - 1) as i:
                with pe.Fori(0, UPS) as k:
                    def tokens(n, tile):
                        return stream[:, n, tile // HALVES,
                                      bass.ds(i * CT + (CT + tile % HALVES * P), P)]

                    def taken():
                        pe.wait_ge(job_taken, i * UPS + k + 1)

                    steps(i * CITERS + k, lambda u: job(i * JOBS + k, u, tokens, True, True, taken))
                with pe.Fori(0, GATE_ITERS) as k:
                    steps(i * CITERS + k + UPS)
                with pe.Fori(0, C) as c:
                    def out(r, start, stop, free=None):
                        def units(n, tile):
                            return hidden[:, bass.ds(r * 2 + n, 1), tile * P:(tile + 1) * P
                                          ].rearrange("p a n -> p (a n)")

                        steps(i * CITERS + c * OUTS + r + (UPS + GATE_ITERS),
                              lambda u: job(i * JOBS + c * OUTS + r + UPS, u, units, start, stop, free))

                    def ready():
                        pe.wait_ge(expert_out, i * E + 2 * E)
                        pe.wait_ge(x2_out, i * C + c + C)

                    out(0, True, False, ready)
                    with pe.Fori(1, OUTS - 1) as r:
                        out(r, False, False)
                    out(OUTS - 1, False, True)
                with pe.Fori(0, REST_ITERS) as k:
                    steps(i * CITERS + k + (CITERS - REST_ITERS))
                pe.wait_ge(hid, i * CT + CT + 1)
                finish(i + 1)
                pe.wait_ge(xz_out, i * NXZ + 2 * NXZ)
            with pe.Fori(0, CITERS) as k:
                steps(k + (CHUNKS - 1) * CITERS)


_INS = ("x", "small", "wkv", "wq", "wproj", "moe", "wu", "we", "wproj2", "wx",
        "wh", "bias_z")


def kernel(**inputs):
    import numpy as np
    import concourse.bacc as bacc
    from concourse.bass_utils import run_bass_kernel_spmd

    a = {k: np.asarray(v) for k, v in inputs.items()}

    def fold_rows(w):
        n = w.shape[1]
        return w.reshape(4, 2, 32, n).transpose(0, 2, 1, 3).reshape(P, C, n)

    def fold_cols(w):
        n = w.shape[0]
        return w.reshape(n, 4, 2, 32).transpose(0, 2, 1, 3).reshape(n, D)

    def plain_rows(w):
        return w.reshape(-1, P, w.shape[1]).transpose(1, 0, 2)

    def vector(v):
        return plain_rows(v.reshape(-1, 1))[:, :, 0]

    f = np.float32
    heads = (np.arange(D)[:, None] // (D // HEADS) == np.arange(HEADS)[None, :]).astype(f)
    before = (np.arange(E)[None, :] < np.arange(E)[:, None]).astype(f).reshape(1, E * E)
    parts = {
        "cond": fold_rows(a["cond_1024"].T),
        "b_q": vector(a["L0_cond_b_q"]),
        "b_kv": vector(a["L0_cond_b_kv"]),
        "no_k": vector(a["L0_cond_no_op_k"].reshape(-1)),
        "no_v": vector(a["L0_cond_no_op_v"].reshape(-1)),
        "b_proj": fold_rows(a["L0_cond_b_proj"].reshape(D, 1)),
        "b_proj2": vector(a["L2_cond_b_proj"]),
        "router": fold_rows(a["L1_cond_router_w"].T),
        "router_t": fold_rows(a["L1_cond_router_t_w"].T),
        "router_bias": np.broadcast_to(a["L1_cond_router_bias"][None, :], (P, E)),
        "head": plain_rows(heads),
        "before": np.broadcast_to(before, (P, E * E)),
        "ident": np.eye(P, 16, dtype=f),
    }
    ups = []
    for m in range(MS):
        for name in ("L1_cond_sw1", "L1_cond_sw3"):
            ups.append(fold_rows(a[name][m * P:(m + 1) * P].T))
    for e in range(E):
        ups.append(fold_rows(a["L1_cond_rw1"].reshape(E, P, D)[e].T))
    down = [plain_rows(fold_cols(a["L1_cond_sw2"].T))]
    down += [fold_cols(w.T)[:, None, :] for w in a["L1_cond_rw2"]]
    down = np.concatenate(down, axis=1)
    downs = [down[:, :, c * P:(c + 1) * P] for c in range(C)]
    arrays = {
        "x": a["x"].reshape(B, T, 4, 2, 32).transpose(2, 4, 3, 0, 1).reshape(P, C, B, T),
        "small": np.concatenate([parts[n].reshape(P, -1) for n in SMALL], axis=1),
        "wkv": fold_rows(a["L0_cond_W_kv"]),
        "wq": plain_rows(fold_cols(a["L0_cond_W_q"].T)),
        "wproj": plain_rows(fold_cols(a["L0_cond_W_proj"])),
        "moe": np.concatenate(ups + downs, axis=1),
        "wu": plain_rows(fold_cols(a["L2_cond_weight_matrix"][:D])),
        "we": fold_rows(fold_cols(a["L2_cond_weight_matrix"][D:])),
        "wproj2": fold_rows(a["L2_cond_W_proj"]),
        "wx": fold_rows(a["L3_cond_Wx"]),
        "wh": fold_rows(a["L3_cond_Wh"]),
        "bias_z": np.broadcast_to(a["L3_cond_b"][None, :], (P, G4)),
    }
    nc = bacc.Bacc("TRN2", target_bir_lowering=False, num_devices=1)
    feed, args = {}, []
    for name in _INS:
        v = np.ascontiguousarray(arrays[name])
        feed[f"in_{name}"] = v
        args.append(nc.dram_tensor(f"in_{name}", v.shape, mybir.dt.from_np(v.dtype), kind="ExternalInput").ap())
    args.append(nc.dram_tensor("out_y", (P, C, B, T), F32, kind="ExternalOutput").ap())
    cond_stack_kernel(nc, *args)
    r = run_bass_kernel_spmd(nc, [feed], core_ids=[0])
    y = r.results[0]["out_y"]
    return np.ascontiguousarray(
        y.reshape(4, 32, C, B, T).transpose(3, 4, 0, 2, 1).reshape(B, T, D))
```

```python
from contextlib import ExitStack

import concourse.bass as bass
from concourse import mybir

F32 = mybir.dt.float32
ALU = mybir.AluOpType
ACT = mybir.ActivationFunctionType
AX = mybir.AxisListType

P = 128
B, T, D = 2, 1024, 256
C = D // P
HEADS = 16
HS = 512
MS = HS // P
E = 8
G4 = 4 * D
TOP_K = 2
EPS = 1e-9

CT = 256
CHUNKS = T // CT
NT = B * CT
Q = NT // P
HALVES = CT // P
XZ_COLS = 512
NXZ = Q * (G4 // XZ_COLS)

U_COLS = 64
Q_ORDER = tuple(range(0, Q, HALVES)) + tuple(q for q in range(Q) if q % HALVES)
FIRST_XZ_BANKS = (0, 1, 2, 7, 5, 6, 3, 4)
XZ_BANKS = (7, 0, 1, 2, 3, 4)
LIN_BANKS = (4, 7)

U = 8
HU = U // 2
J = 4
HC = D // J
GI, GF, GO, GC = 0, 1, 2, 3
CITERS = CT // U
STORES = 2

UPS = E + 2 * MS
UNITS = MS + E
OUTS = UNITS // 2
JOBS = UPS + C * OUTS
DOWN = 2 * UPS
SIDE_XZ = 2
assert HU == Q and C == 2 and JOBS + C + SIDE_XZ == CITERS

SMALL = {}


def _pack_small():
    at = 0
    for name, width in (("cond", C * B), ("b_q", C), ("b_kv", 2 * C), ("no_k", C), ("no_v", C),
                        ("b_proj", C), ("b_proj2", C), ("router", C * E), ("router_t", C * E),
                        ("router_bias", E), ("head", C * HEADS), ("before", E * E), ("ident", 16)):
        SMALL[name] = (at, at + width)
        at += width
    return at


N_SMALL = _pack_small()


def cond_stack_kernel(nc, x, small, wkv, wq, wproj, moe, wu, we, wproj2, wx, wh, bias_z, y):
    ctx = ExitStack()
    with ctx:
        def sb(name, shape):
            return ctx.enter_context(nc.sbuf_tensor(name, shape, F32))

        def sem(name):
            return ctx.enter_context(nc.semaphore(name))

        xz_dram = nc.dram_tensor("xz_scratch", (B, T, G4), F32).ap()
        comb_dram = nc.dram_tensor("comb_scratch", (CHUNKS, NT * E), F32).ap()

        small_sb = sb("small_sb", [P, N_SMALL])
        wkv_sb = sb("wkv_sb", [P, C, 2 * D])
        wq_sb = sb("wq_sb", [P, C, D])
        wproj_sb = sb("wproj_sb", [P, C, D])
        moe_sb = sb("moe_sb", [P, 2 * JOBS, P])
        wu_sb = sb("wu_sb", [P, C, D])
        we_sb = sb("we_sb", [P, C, D])
        wproj2_sb = sb("wproj2_sb", [P, C, D])
        wx_sb = sb("wx_sb", [P, C, G4])
        wh_sb = sb("wh_sb", [P, C, G4])
        bias_z_sb = sb("bias_z_sb", [P, G4])

        def part(name, pattern=None, **kw):
            ap = small_sb[:, SMALL[name][0]:SMALL[name][1]]
            return ap.rearrange(pattern, **kw) if pattern else ap

        cond = part("cond", "p (c b) -> p c b", c=C)
        b_q = part("b_q")
        b_kv = part("b_kv")
        no_k, no_v = part("no_k"), part("no_v")
        b_proj, b_proj2 = part("b_proj"), part("b_proj2")
        router = part("router", "p (c e) -> p c e", c=C)
        router_t = part("router_t", "p (c e) -> p c e", c=C)
        router_bias = part("router_bias")
        head = part("head", "p (c h) -> p c h", c=C)
        before = part("before", "p (e f) -> p e f", e=E)
        ident = part("ident")

        stream = sb("stream", [P, C, B, T])

        kv = sb("kv", [P, 2 * C, B])
        k_diff = sb("k_diff", [P, C, B])
        v_diff = sb("v_diff", [P, C, B])
        k_heads = sb("k_heads", [P, C, B, HEADS])
        v_heads = sb("v_heads", [P, C, B, HEADS])
        score_w = sb("score_w", [P, C, B, HEADS])
        score_b = sb("score_b", [HEADS, B])
        value_w = sb("value_w", [HEADS, B, D])
        attn_b = sb("attn_b", [P, C])
        cond_rep = sb("cond_rep", [P, C, B, P])
        u_act = sb("u_act", [P, C, B])
        route_t = sb("route_t", [P, B, E])
        cond_out = sb("cond_out", [P, C, B])

        w1 = sb("w1", [HEADS, B, CT])
        x1 = sb("x1", [P, C, NT])
        x2 = sb("x2", [P, C, NT])
        x3 = sb("x3", [P, C, NT])
        s_in = sb("s_in", [P, Q, E])
        s_all = sb("s_all", [P, Q, E])
        sel = sb("sel", [P, Q, E])
        beats = sb("beats", [P, Q, E, E])
        ties = sb("ties", [P, Q, E, E])
        rank = sb("rank", [P, Q, E])
        s_top = sb("s_top", [P, Q, E])
        top = sb("top", [P, Q, E])
        den = sb("den", [P, Q])
        den_eps = sb("den_eps", [P, Q])
        den_inv = sb("den_inv", [P, Q])
        den_ok = sb("den_ok", [P, Q])
        inv_ok = sb("inv_ok", [P, Q])
        half_bad = sb("half_bad", [P, Q])
        comb_a = sb("comb_a", [P, Q, E])
        comb_b = sb("comb_b", [P, Q, E])
        comb = sb("comb", [P, Q, E])
        comb_all = sb("comb_all", [P, NT, E])
        sig = sb("sig", [P, 2, NT])
        gated = sb("gated", [P, 2, NT])
        gate_in = sb("gate_in", [P, NT])
        hidden = sb("hidden", [P, UNITS, NT])
        xz_sb = sb("xz_sb", [P, Q, G4])

        staged = sb("staged", [P, 2, 4, D])
        blocks = sb("blocks", [P, 2, P])
        h_ring = sb("h_ring", [P, U, C, B])
        if_act = sb("if_act", [P, 2, 2, C * B, 2])
        o_act = sb("o_act", [P, 2, C * B])

        bank = [ctx.enter_context(nc.psum_tensor(f"bank{n}", [P, 512], F32)) for n in range(8)]

        t_if_b = bank[3][:, 0:3 * HC].rearrange("p (g c r) -> p g c r", g=3, r=32)
        t_c_b = bank[4][:, 0:HC].rearrange("p (c r) -> p c r", r=32)
        cell_b = bank[5][:, 0:4 * C * B].rearrange("p (v q k) -> p v q k", v=2, k=2)
        g_pairs = bank[6][:, 0:4 * C * B].rearrange("p (v q k) -> p v q k", v=2, k=2)
        c_tanh = bank[6][:, 4 * C * B:6 * C * B].rearrange("p (v q) -> p v q", v=2)

        small_in = sem("small_in")
        x_in = [sem(f"x_in{i}") for i in range(CHUNKS)]
        w_in = {n: sem(f"{n}_in") for n in ("wkv", "wq", "wproj", "up", "down", "wu", "we", "wproj2",
                                            "wx", "wh", "bias_z")}
        kv_made = sem("kv_made")
        kv_out = sem("kv_out")
        diff_made = sem("diff_made")
        heads_made = sem("heads_made")
        u_made = sem("u_made")
        u_out = sem("u_out")
        rep_made = sem("rep_made")
        score_made = sem("score_made")
        score_out = sem("score_out")
        value_made = sem("value_made")
        value_out = sem("value_out")
        term_made = sem("term_made")
        term_out = sem("term_out")
        cond_made = sem("cond_made")
        cond_done = sem("cond_done")
        d_made = sem("d_made")
        w1_out = sem("w1_out")
        attn_made = sem("attn_made")
        x1_out = sem("x1_out")
        x1_kept = sem("x1_kept")
        route_made = sem("route_made")
        s_in_out = sem("s_in_out")
        s_out = sem("s_out")
        top_step = sem("top_step")
        comb_out = sem("comb_out")
        comb_stored = sem("comb_stored")
        comb_in = sem("comb_in")
        up_made = sem("up_made")
        sig_out = sem("sig_out")
        gated_out = sem("gated_out")
        shared_out = sem("shared_out")
        hid_made = sem("hid_made")
        gelu_out = sem("gelu_out")
        expert_out = sem("expert_out")
        moe_made = sem("moe_made")
        x2_out = sem("x2_out")
        lin_made = sem("lin_made")
        x3_out = sem("x3_out")
        x3_kept = sem("x3_kept")
        xz_made = sem("xz_made")
        xz_out = sem("xz_out")
        xz_stored = [sem(f"xz_stored{q}") for q in range(Q)]
        z_if = sem("z_if")
        z_c = sem("z_c")
        z_o = sem("z_o")
        t_if = sem("t_if")
        t_c = sem("t_c")
        t_o = sem("t_o")
        a_if = sem("a_if")
        a_c = sem("a_c")
        a_o = sem("a_o")
        kept = sem("kept")
        cell = sem("cell")
        cell_tanh = sem("cell_tanh")
        hid = sem("hid")
        staged_clear = sem("staged_clear")
        staged_in = [sem(f"staged_in{n}") for n in range(2)]
        staged_used = [sem(f"staged_used{n}") for n in range(2)]
        added = sem("added")
        block_in = [sem(f"block_in{n}") for n in range(2)]
        block_used = [sem(f"block_used{n}") for n in range(2)]
        expert_taken = sem("expert_taken")
        gate_taken = sem("gate_taken")
        unit_taken = sem("unit_taken")
        side_sig = sem("side_sig")
        side_gated = sem("side_gated")
        side_gelu = sem("side_gelu")
        y_stored = sem("y_stored")

        block = ctx.enter_context(nc.Block())

        @block.sync
        def _(sp):
            sp.dma_start(small_sb[:, :], small).then_inc(small_in, 16)
            for name, dst, src in (("wkv", wkv_sb, wkv), ("wq", wq_sb, wq)):
                sp.dma_start(dst[:], src).then_inc(w_in[name], 16)
            sp.dma_start(stream[:, :, :, 0:CT], x[:, :, :, 0:CT]).then_inc(x_in[0], 16)
            for name, dst, src in (("wproj", wproj_sb, wproj),
                                   ("up", moe_sb[:, 0:DOWN, :], moe[:, 0:DOWN, :]),
                                   ("wproj2", wproj2_sb, wproj2), ("wu", wu_sb, wu),
                                   ("down", moe_sb[:, DOWN:, :], moe[:, DOWN:, :]), ("we", we_sb, we),
                                   ("wx", wx_sb, wx), ("bias_z", bias_z_sb, bias_z), ("wh", wh_sb, wh)):
                sp.dma_start(dst[:], src).then_inc(w_in[name], 16)

            def keep_gates(m):
                sp.wait_ge(comb_out, m + 1)
                sp.dma_start(comb_dram[m:m + 1, :].rearrange("a (q p e) -> p (a q) e", q=Q, e=E),
                             comb[:, :, :]).then_inc(comb_stored, 16)

            def spread(m):
                sp.dma_start(comb_all[:, :, :].rearrange("p n e -> p (n e)"),
                             comb_dram[bass.ds(m, 1), :].partition_broadcast(P).rearrange("p a n -> p (a n)")
                             ).then_inc(comb_in, 16)

            def gate_inputs(m):
                rows = [sp.snap(m * CT + half * P) for half in range(HALVES)]
                tiles = [sp.snap(m * NXZ + 2 * (at + 1)) for at in range(Q)]
                for at, q in enumerate(Q_ORDER):
                    b, half = q // HALVES, q % HALVES
                    sp.wait_ge(xz_out, tiles[at])
                    if half == 0:
                        for n in range(2):
                            sp.dma_start(staged[b * HU:(b + 1) * HU, n, :, :].rearrange("p g d -> p (g d)"),
                                         xz_sb[n * HU:(n + 1) * HU, q, :]).then_inc(staged_in[n], 16)
                    sp.dma_start(xz_dram[b, bass.ds(rows[half], P), :],
                                 xz_sb[:, q, :]).then_inc(xz_stored[q], 16)

            def gate_inputs_stored(m):
                stored = sp.snap(m * 16 + 32)
                for q in range(Q):
                    sp.wait_ge(xz_stored[q], stored)

            def stage(used, n, at):
                sp.wait_ge(staged_used[n], used)
                for b in range(B):
                    sp.dma_start(staged[b * HU:(b + 1) * HU, n, :, :].rearrange("p g d -> p (g d)"),
                                 xz_dram[b, bass.ds(at, HU), :]).then_inc(staged_in[n], 16)

            def bring(used, n, block_):
                sp.wait_ge(block_used[n], used)
                sp.dma_start(blocks[:, n, :], moe_sb[:, bass.ds(block_, 1), :].rearrange("p a n -> p (a n)")
                             ).then_inc(block_in[n], 16)

            def rounds(i, first, length, job=None):
                with sp.Fori(0, length) as k:
                    at = [sp.snap(i * CT + k * U + (first * U + U + n * HU)) for n in range(2)]
                    used = sp.snap(i * CITERS + k + (first + 1))
                    if job is not None:
                        jobs = sp.snap(i * JOBS + k + (job + 1))
                        block_ = [sp.snap(k * 2 + (2 * job + n)) for n in range(2)]
                    for n in range(2):
                        stage(used, n, at[n])
                        if job is not None:
                            bring(jobs, n, block_[n])

            per_store = CITERS // STORES

            def store(i, piece):
                at = sp.snap(i * CT + piece * per_store * U)
                count = sp.snap(i * CITERS + ((piece + 1) * per_store + 1))
                sp.wait_ge(added, count)
                sp.dma_start(y[:, :, :, bass.ds(at, per_store * U)],
                             stream[:, :, :, bass.ds(at, per_store * U)]).then_inc(y_stored, 16)

            keep_gates(0)
            sp.wait_ge(comb_stored, 32)
            spread(0)
            for m in range(1, CHUNKS):
                keep_gates(m)
            sp.wait_ge(w_in["up"], 16)
            for n in range(2):
                bring(1, n, n)
            sp.wait_ge(staged_clear, 1)
            gate_inputs(0)
            with sp.Fori(0, CHUNKS - 1) as i:
                chunk_, scaled = sp.snap(i + 1), sp.snap(i * E + E)
                gate_inputs_stored(i)
                sp.wait_ge(w_in["down"], 16)
                sp.wait_ge(comb_stored, 16 * (CHUNKS + 1))
                sp.wait_ge(expert_out, scaled)
                spread(chunk_)
                assert per_store == UPS
                rounds(i, 0, UPS, 1)
                store(i, 0)
                rounds(i, UPS, C * OUTS - 1, UPS + 1)
                rounds(i, JOBS - 1, C + SIDE_XZ)
                jobs = sp.snap(i * JOBS + (JOBS + 1))
                for n in range(2):
                    bring(jobs, n, n)
                store(i, 1)
                used = sp.snap(i * CITERS + CITERS)
                for n in range(2):
                    sp.wait_ge(staged_used[n], used)
                gate_inputs(i + 1)
            gate_inputs_stored(CHUNKS - 1)
            for piece in range(STORES):
                rounds(CHUNKS - 1, piece * per_store, per_store - piece)
                store(CHUNKS - 1, piece)
            sp.wait_ge(y_stored, 16 * STORES * CHUNKS)

        @block.gpsimd
        def _(pool):
            pool.sem_inc(x3_kept, 1)
            for q in range(Q):
                pool.sem_inc(xz_stored[q], 16)
            pool.sem_inc(added, 1)
            for free in (t_if, t_c, t_o):
                pool.sem_inc(free, 1)
            pool.sem_inc(comb_stored, 16)
            pool.sem_inc(x1_kept, 1)
            for n in range(2):
                pool.sem_inc(block_used[n], 1)
            pool.sem_inc(expert_taken, 1)
            pool.sem_inc(unit_taken, 1)
            pool.memset(staged[:, :, :, :], 0.0).then_inc(staged_clear, 1)
            with pool.Fori(0, CHUNKS) as i:
                pool.wait_ge(x1_out, i * C + C)
                pool.tensor_copy(stream[:, :, :, bass.ds(i * CT, CT)],
                                 x1[:, :, :].rearrange("p c (b t) -> p c b t", b=B)).then_inc(x1_kept, 1)

            def keep(m):
                pool.wait_ge(x3_out, m * (C * B) + C * B)
                pool.tensor_copy(stream[:, :, :, bass.ds(m * CT, CT)],
                                 x3[:, :, :].rearrange("p c (b t) -> p c b t", b=B)).then_inc(x3_kept, 1)

            def add(m, it):
                pool.wait_ge(x3_kept, m + 2)
                pool.wait_ge(hid, it * U + U + 1)
                out = stream[:, :, :, bass.ds(it * U, U)].rearrange("p c b t -> p (c b) t")
                pool.tensor_tensor(out, out, h_ring[:, :, :, :].rearrange("p u c b -> p (c b) u"),
                                   ALU.add).then_inc(added, 1)

            keep(0)
            with pool.Fori(0, CHUNKS - 1) as i:
                with pool.Fori(0, CITERS) as k:
                    add(i, i * CITERS + k)
                keep(i + 1)
            with pool.Fori(0, CITERS) as k:
                add(CHUNKS - 1, k + (CHUNKS - 1) * CITERS)

        @block.scalar
        def _(act):
            act.wait_ge(w_in["wq"], 16)
            for i in range(1, CHUNKS):
                times = slice(i * CT, (i + 1) * CT)
                act.dma_start(stream[:, :, :, times], x[:, :, :, times]).then_inc(x_in[i], 16)
            act.preload_act_table_set("sigmoid_and_others")
            act.wait_ge(small_in, 16)

            def weigh(i):
                act.wait_ge(d_made, i + 1)
                if i > 0:
                    act.wait_ge(attn_made, i * C)
                for b in range(B):
                    nc.scalar.activation(w1[:, b, :], bank[0][0:HEADS, b * CT:(b + 1) * CT], ACT.Sigmoid,
                                         bias=score_b[:, b:b + 1]).then_inc(w1_out, 1)

            def gate(i):
                act.wait_ge(s_in_out, i + 1)
                if i > 0:
                    act.wait_ge(comb_out, i)
                nc.scalar.activation(s_all[:, :, :].rearrange("p q e -> p (q e)"),
                                     s_in[:, :, :].rearrange("p q e -> p (q e)"), ACT.Sigmoid).then_inc(s_out, 1)

            def shared_gate(m):
                act.wait_ge(up_made, m + 1)
                if m >= 2:
                    act.wait_ge(gated_out, m - 1)
                nc.scalar.activation(sig[:, m % 2, :], bank[4 + 2 * (m % 2)][:, :],
                                     ACT.Sigmoid).then_inc(sig_out, 1)

            act.wait_ge(score_out, 2)
            weigh(0)
            gate(0)
            weigh(1)
            shared_gate(0)
            shared_gate(1)
            gate(1)
            weigh(2)
            shared_gate(2)
            shared_gate(3)
            gate(2)
            weigh(3)
            act.wait_ge(u_made, 1)
            for m in range(C):
                nc.scalar.activation(u_act[:, m, :], bank[3][:, U_COLS + m * B:U_COLS + (m + 1) * B], ACT.Gelu,
                                     bias=b_proj2[:, m:m + 1]).then_inc(u_out, 1)
            for e in range(E):
                act.wait_ge(hid_made, e + 1)
                nc.scalar.activation(hidden[:, MS + e, :], bank[4 + e % 4][:, :], ACT.Gelu).then_inc(gelu_out, 1)
            gate(3)

            def steps(it, side=None):
                begun = [act.snap(it * U + u + 2) for u in range(U)]
                for u in range(U):
                    if side and u in side:
                        side[u]()
                    par, now = u % 2, begun[u]
                    act.wait_ge(t_if, now)
                    nc.scalar.activation(if_act[:, par, :, :, 0], t_if_b[:, 0:2, :, 0:B],
                                         ACT.Sigmoid).then_inc(a_if, 1)
                    act.wait_ge(t_c, now)
                    nc.scalar.activation(g_pairs[:, par, :, 1], t_c_b[:, :, 0:B], ACT.Tanh).then_inc(a_c, 1)
                    act.wait_ge(t_o, now)
                    nc.scalar.activation(o_act[:, par, :], t_if_b[:, 2, :, 0:B], ACT.Sigmoid).then_inc(a_o, 1)
                    act.wait_ge(cell, now)
                    nc.scalar.activation(c_tanh[:, par, :], cell_b[:, par, :, 1],
                                         ACT.Tanh).then_inc(cell_tanh, 1)

            act.preload_act_table_set("sigmoid_and_others")
            with act.Fori(0, CHUNKS - 1) as i:
                with act.Fori(0, E) as e:
                    def take_expert():
                        act.wait_ge(block_used[1], i * JOBS + e + 2)
                        nc.scalar.activation(hidden[:, bass.ds(e + MS, 1), :].rearrange("p a n -> p (a n)"),
                                             bank[7][:, :], ACT.Copy).then_inc(expert_taken, 1)

                    steps(i * CITERS + e, {U - 1: take_expert})
                act.wait_ge(expert_taken, i * E + E + 1)
                nc.scalar.activation(hidden[:, MS:UNITS, :], hidden[:, MS:UNITS, :],
                                     ACT.Gelu).then_inc(side_gelu, 1)
                act.preload_act_table_set("sigmoid_and_others")
                with act.Fori(0, MS) as m:
                    def take_gate():
                        act.wait_ge(block_used[1], i * JOBS + m * 2 + (E + 2))
                        nc.scalar.activation(gate_in[:, :], bank[7][:, :], ACT.Copy).then_inc(gate_taken, 1)

                    def side_sigmoid():
                        act.wait_ge(gate_taken, i * MS + m + 1)
                        nc.scalar.activation(sig[:, 0, :], gate_in[:, :], ACT.Sigmoid).then_inc(side_sig, 1)

                    steps(i * CITERS + m * 2 + E, {U - 1: take_gate})
                    steps(i * CITERS + m * 2 + (E + 1), {0: side_sigmoid})
                with act.Fori(0, CITERS - UPS) as k:
                    steps(i * CITERS + k + UPS)
            with act.Fori(0, CITERS) as k:
                steps(k + (CHUNKS - 1) * CITERS)

        @block.vector
        def _(dve):
            def pairs(ap):
                return ap.unsqueeze(2).to_broadcast([P, C, B])

            dve.wait_ge(small_in, 16)
            nc.vector.tensor_copy(cond_rep[:, :, :, :],
                                  cond.unsqueeze(3).to_broadcast([P, C, B, P])).then_inc(rep_made, 1)
            dve.wait_ge(kv_made, 1)
            nc.vector.tensor_tensor(kv[:, :, :], bank[0][:, 0:2 * C * B].rearrange("p (m b) -> p m b", b=B),
                                    b_kv.unsqueeze(2).to_broadcast([P, 2 * C, B]), ALU.add).then_inc(kv_out, 1)
            dve.wait_ge(kv_out, 1)
            nc.vector.tensor_tensor(k_diff[:, :, :], kv[:, 0:C, :], pairs(no_k), ALU.subtract).then_inc(diff_made, 1)
            nc.vector.tensor_tensor(v_diff[:, :, :], kv[:, C:2 * C, :], pairs(no_v),
                                    ALU.subtract).then_inc(diff_made, 1)
            dve.wait_ge(diff_made, 2)
            for dst, src in ((k_heads, k_diff), (v_heads, v_diff)):
                for m in range(C):
                    nc.vector.tensor_tensor(dst[:, m, :, :],
                                            head[:, m, :].unsqueeze(1).to_broadcast([P, B, HEADS]),
                                            src[:, m, :].unsqueeze(2).to_broadcast([P, B, HEADS]),
                                            ALU.mult).then_inc(heads_made, 1)
            dve.wait_ge(score_made, 1)
            nc.vector.tensor_copy(score_w[:, :, :, :].rearrange("p c b h -> p (c b h)"),
                                  bank[1][:, 0:C * B * HEADS]).then_inc(score_out, 1)
            nc.vector.tensor_copy(score_b[:, :], bank[2][0:HEADS, 0:B]).then_inc(score_out, 1)
            dve.wait_ge(value_made, 1)
            nc.vector.tensor_copy(value_w[:, :, :].rearrange("h b d -> h (b d)"),
                                  bank[3][0:HEADS, :]).then_inc(value_out, 1)
            dve.wait_ge(value_made, 2)
            nc.vector.tensor_tensor(attn_b[:, :], bank[4][:, 0:C], b_proj, ALU.add).then_inc(value_out, 1)
            dve.wait_ge(value_out, 2)

            def attended(i):
                dve.wait_ge(x1_kept, i + 1)
                if i > 0:
                    dve.wait_ge(route_made, i)
                dve.wait_ge(x_in[i], 16)
                for c in range(C):
                    dve.wait_ge(attn_made, i * C + c + 1)
                    nc.vector.scalar_tensor_tensor(
                        out=x1[:, c, :].rearrange("p (b t) -> p b t", b=B),
                        in0=bank[1 + c][:, :].rearrange("p (b t) -> p b t", b=B), scalar=attn_b[:, c:c + 1],
                        in1=stream[:, c, :, i * CT:(i + 1) * CT], op0=ALU.add, op1=ALU.add).then_inc(x1_out, 1)

            def route(i):
                if i == 0:
                    dve.wait_ge(term_made, 1)
                    nc.vector.tensor_copy(route_t[:, :, :].rearrange("p b e -> p (b e)"),
                                          bank[5][:, 0:B * E]).then_inc(term_out, 1)
                    dve.wait_ge(term_out, 1)
                else:
                    dve.wait_ge(s_out, i)
                dve.wait_ge(route_made, i + 1)
                nc.vector.tensor_tensor(
                    s_in[:, :, :].rearrange("p (b h) e -> p b h e", b=B),
                    bank[3][:, 0:Q * E].rearrange("p (b h e) -> p b h e", b=B, h=HALVES),
                    route_t[:, :, :].unsqueeze(2).to_broadcast([P, B, HALVES, E]), ALU.add).then_inc(s_in_out, 1)

            def gates(i):
                steps = 11
                done = [0]

                def step(ins):
                    done[0] += 1
                    ins.then_inc(top_step, 1)
                    dve.wait_ge(top_step, i * steps + done[0])

                rivals = sel[:, :, :].unsqueeze(2).to_broadcast([P, Q, E, E])
                own = sel[:, :, :].unsqueeze(3).to_broadcast([P, Q, E, E])
                dve.wait_ge(s_out, i + 1)
                step(nc.vector.tensor_tensor(sel[:, :, :], s_all[:, :, :],
                                             router_bias.unsqueeze(1).to_broadcast([P, Q, E]), ALU.add))
                nc.vector.tensor_tensor(beats[:, :, :, :], rivals, own, ALU.is_gt)
                step(nc.vector.tensor_tensor(ties[:, :, :, :], rivals, own, ALU.is_equal))
                step(nc.vector.tensor_tensor(ties[:, :, :, :], ties[:, :, :, :],
                                             before.unsqueeze(1).to_broadcast([P, Q, E, E]), ALU.mult))
                step(nc.vector.tensor_tensor(beats[:, :, :, :], beats[:, :, :, :], ties[:, :, :, :], ALU.add))
                step(nc.vector.tensor_reduce(rank[:, :, :], beats[:, :, :, :], AX.X, ALU.add))
                nc.vector.tensor_scalar(top[:, :, :], rank[:, :, :], float(TOP_K), None, ALU.is_lt)
                step(nc.vector.scalar_tensor_tensor(out=s_top[:, :, :], in0=rank[:, :, :], scalar=float(TOP_K),
                                                    in1=s_all[:, :, :], op0=ALU.is_lt, op1=ALU.mult))
                step(nc.vector.tensor_reduce(den[:, :], s_top[:, :, :], AX.X, ALU.add))
                nc.vector.tensor_scalar(den_ok[:, :], den[:, :], EPS, None, ALU.is_gt)
                step(nc.vector.tensor_scalar(den_eps[:, :], den[:, :], EPS, None, ALU.add))
                nc.vector.tensor_scalar(half_bad[:, :], den_ok[:, :], -1.0 / TOP_K, 1.0 / TOP_K, ALU.mult, ALU.add)
                step(nc.vector.reciprocal(den_inv[:, :], den_eps[:, :]))
                nc.vector.tensor_tensor(comb_b[:, :, :], top[:, :, :],
                                        half_bad[:, :].unsqueeze(2).to_broadcast([P, Q, E]), ALU.mult)
                step(nc.vector.tensor_tensor(inv_ok[:, :], den_inv[:, :], den_ok[:, :], ALU.mult))
                step(nc.vector.tensor_tensor(comb_a[:, :, :], s_top[:, :, :],
                                             inv_ok[:, :].unsqueeze(2).to_broadcast([P, Q, E]), ALU.mult))
                dve.wait_ge(comb_stored, i * 16 + 16)
                nc.vector.tensor_tensor(comb[:, :, :], comb_a[:, :, :], comb_b[:, :, :],
                                        ALU.add).then_inc(comb_out, 1)
                assert done[0] == steps

            def shared_units(m):
                pair = 4 + 2 * (m % 2)
                dve.wait_ge(sig_out, m + 1)
                nc.vector.tensor_tensor(gated[:, m % 2, :], sig[:, m % 2, :], bank[pair][:, :],
                                        ALU.mult).then_inc(gated_out, 1)
                dve.wait_ge(gated_out, m + 1)
                nc.vector.tensor_tensor(hidden[:, m, :], gated[:, m % 2, :], bank[pair + 1][:, :],
                                        ALU.mult).then_inc(shared_out, 1)

            def scale(e):
                nc.vector.tensor_tensor(hidden[:, MS + e, :], hidden[:, MS + e, :], comb_all[:, :, e],
                                        ALU.mult).then_inc(expert_out, 1)

            def layer2(m, c, src):
                nc.vector.scalar_tensor_tensor(out=x2[:, c, :].rearrange("p (b t) -> p b t", b=B),
                                               in0=src[:, :].rearrange("p (b t) -> p b t", b=B),
                                               scalar=1.0 / (1 + TOP_K),
                                               in1=stream[:, c, :, bass.ds(m * CT, CT)], op0=ALU.mult,
                                               op1=ALU.add).then_inc(x2_out, 1)

            def layer3(m, c, src):
                dve.wait_ge(x3_kept, m + 1)
                dve.wait_ge(lin_made, m * C + c + 1)
                for b in range(B):
                    cols = slice(b * CT, (b + 1) * CT)
                    nc.vector.scalar_tensor_tensor(out=x3[:, c, cols], in0=src[:, cols],
                                                   scalar=cond_out[:, c, b:b + 1], in1=x2[:, c, cols],
                                                   op0=ALU.add, op1=ALU.add).then_inc(x3_out, 1)

            def gate_inputs(m, first):
                for n in range(first, NXZ):
                    b = XZ_BANKS[n - first] if first else FIRST_XZ_BANKS[n]
                    q, g = Q_ORDER[n // 2], n % 2
                    cols = slice(g * XZ_COLS, (g + 1) * XZ_COLS)
                    if g == 0:
                        dve.wait_ge(xz_stored[q], m * 16 + 16)
                    dve.wait_ge(xz_made, m * NXZ + n + 1)
                    nc.vector.tensor_tensor(xz_sb[:, q, cols], bank[b][:, :], bias_z_sb[:, cols],
                                            ALU.add).then_inc(xz_out, 1)

            def scale_made(e):
                dve.wait_ge(gelu_out, e + 1)
                scale(e)

            attended(0)
            route(0)
            gates(0)
            shared_units(0)
            attended(1)
            shared_units(1)
            route(1)
            gates(1)
            shared_units(2)
            attended(2)
            shared_units(3)
            route(2)
            gates(2)
            attended(3)
            dve.wait_ge(cond_made, 1)
            nc.vector.tensor_copy(cond_out[:, :, :].rearrange("p c b -> p (c b)"),
                                  bank[3][:, U_COLS + C * B:U_COLS + 2 * C * B]).then_inc(cond_done, 1)
            dve.wait_ge(comb_in, 16)
            for e in range(5):
                scale_made(e)
            route(3)
            for e in range(5, E):
                scale_made(e)
            gates(3)
            dve.wait_ge(x1_kept, CHUNKS + 1)
            for c in range(C):
                dve.wait_ge(moe_made, c + 1)
                layer2(0, c, bank[4 + c])
            dve.wait_ge(w_in["bias_z"], 16)
            dve.wait_ge(cond_done, 1)
            for c in range(C):
                layer3(0, c, bank[LIN_BANKS[c]])
            gate_inputs(0, 0)

            dve.wait_ge(xz_out, NXZ)
            nc.vector.memset(bank[6][:, 0:6 * C * B], 0.0)
            nc.vector.memset(bank[5][:, 0:4 * C * B], 0.0).then_inc(cell, 1)
            nc.vector.tensor_copy(h_ring[:, U - 1, :, :], cond).then_inc(hid, 1)

            def steps(it, side=None):
                added_count = dve.snap(it + 1)
                count = [dve.snap(it * U + u + 1) for u in range(U)]
                for u in range(U):
                    if side and u in side:
                        side[u]()
                    par, now = u % 2, count[u]
                    if u == 0:
                        dve.wait_ge(added, added_count)
                    dve.wait_ge(z_if, now)
                    nc.vector.transpose(bank[3][:, 0:2 * HC], bank[0][:, 0:2 * HC]).then_inc(t_if, 1)
                    dve.wait_ge(z_c, now)
                    nc.vector.transpose(bank[4][:, 0:HC], bank[1][:, 0:HC]).then_inc(t_c, 1)
                    dve.wait_ge(a_if, now)
                    nc.vector.tensor_tensor(if_act[:, par, 0, :, 1], if_act[:, par, 1, :, 0],
                                            cell_b[:, 1 - par, :, 1], ALU.mult).then_inc(kept, 1)
                    dve.wait_ge(z_o, now)
                    nc.vector.transpose(bank[3][:, 2 * HC:3 * HC], bank[2][:, 0:HC]).then_inc(t_o, 1)
                    dve.wait_ge(a_c, now)
                    dve.wait_ge(kept, now)
                    nc.vector.tensor_tensor_scan(cell_b[:, par, :, :].rearrange("p q k -> p (q k)"),
                                                 g_pairs[:, par, :, :].rearrange("p q k -> p (q k)"),
                                                 if_act[:, par, 0, :, :].rearrange("p q k -> p (q k)"), 0.0,
                                                 ALU.mult, ALU.add).then_inc(cell, 1)
                    dve.wait_ge(cell_tanh, now)
                    nc.vector.tensor_tensor(h_ring[:, u, :, :].rearrange("p c b -> p (c b)"), o_act[:, par, :],
                                            c_tanh[:, par, :], ALU.mult).then_inc(hid, 1)

            def job_made(i, k):
                dve.wait_ge(block_used[1], i * JOBS + k + 2)

            with dve.Fori(0, CHUNKS - 1) as i:
                with dve.Fori(0, E) as e:
                    steps(i * CITERS + e)
                with dve.Fori(0, MS) as m:
                    def side_scale(n):
                        def run():
                            dve.wait_ge(side_gelu, i + 1)
                            dve.wait_ge(comb_in, i * 16 + 32)
                            units = hidden[:, bass.ds(m * 2 + (MS + n), 1), :].rearrange("p a n -> p (a n)")
                            nc.vector.tensor_tensor(units, units,
                                                    comb_all[:, :, bass.ds(m * 2 + n, 1)
                                                             ].rearrange("p n a -> p (n a)"),
                                                    ALU.mult).then_inc(expert_out, 1)
                        return run

                    def side_gate():
                        dve.wait_ge(side_sig, i * MS + m + 1)
                        nc.vector.tensor_tensor(gated[:, 0, :], sig[:, 0, :], gate_in[:, :],
                                                ALU.mult).then_inc(side_gated, 1)

                    def take_unit():
                        job_made(i, m * 2 + (E + 1))
                        dve.wait_ge(side_gated, i * MS + m + 1)
                        nc.vector.tensor_tensor(hidden[:, bass.ds(m, 1), :].rearrange("p a n -> p (a n)"),
                                                gated[:, 0, :], bank[7][:, :], ALU.mult).then_inc(unit_taken, 1)

                    steps(i * CITERS + m * 2 + E, {3: side_scale(0), 5: side_scale(1)})
                    steps(i * CITERS + m * 2 + (E + 1), {2: side_gate, U - 1: take_unit})
                for c in range(C):
                    def take_out():
                        job_made(i, UPS + c * OUTS + OUTS - 1)
                        layer2(i + 1, c, bank[7])

                    first = UPS + c * OUTS
                    with dve.Fori(0, OUTS - 1) as k:
                        steps(i * CITERS + k + first)
                    steps(i * CITERS + first + OUTS - 1, {U - 1: take_out})
                for c in range(C):
                    steps(i * CITERS + JOBS + c, {U - 1: lambda: layer3(i + 1, c, bank[7])})
                with dve.Fori(0, SIDE_XZ) as g:
                    def take_xz():
                        dve.wait_ge(xz_stored[Q_ORDER[0]], i * 16 + 32)
                        dve.wait_ge(xz_made, i * NXZ + g + (NXZ + 1))
                        cols = bass.ds(g * XZ_COLS, XZ_COLS)
                        nc.vector.tensor_tensor(xz_sb[:, Q_ORDER[0], cols], bank[7][:, :],
                                                bias_z_sb[:, cols], ALU.add).then_inc(xz_out, 1)

                    steps(i * CITERS + g + (JOBS + C), {U - 1: take_xz})
                gate_inputs(i + 1, SIDE_XZ)
                dve.wait_ge(xz_out, i * NXZ + 2 * NXZ)
            with dve.Fori(0, CITERS) as k:
                steps(k + (CHUNKS - 1) * CITERS)

        @block.tensor
        def _(pe):
            pe.wait_ge(small_in, 16)
            pe.wait_ge(w_in["wkv"], 16)
            for m in range(2 * C):
                for c in range(C):
                    last = nc.tensor.matmul(bank[0][:, m * B:(m + 1) * B], wkv_sb[:, c, m * P:(m + 1) * P],
                                            cond[:, c, :], start=(c == 0), stop=(c == C - 1))
            last.then_inc(kv_made, 1)
            pe.wait_ge(w_in["wq"], 16)
            pe.wait_ge(heads_made, C)
            for c in range(C):
                for m in range(C):
                    nc.tensor.matmul(bank[1][:, c * B * HEADS:(c + 1) * B * HEADS],
                                     wq_sb[:, m, c * P:(c + 1) * P],
                                     k_heads[:, m, :, :].rearrange("p b h -> p (b h)"),
                                     start=(m == 0), stop=(m == C - 1))
            for b in range(B):
                for m in range(C):
                    last = nc.tensor.matmul(bank[2][0:HEADS, b:b + 1], k_heads[:, m, b, :], b_q[:, m:m + 1],
                                            start=(m == 0), stop=(m == C - 1))
            last.then_inc(score_made, 1)
            def scores(i):
                pe.wait_ge(x_in[i], 16)
                if i > 0:
                    pe.wait_ge(w1_out, i * B)
                for b in range(B):
                    for c in range(C):
                        last = nc.tensor.matmul(bank[0][0:HEADS, b * CT:(b + 1) * CT], score_w[:, c, b, :],
                                                stream[:, c, b, i * CT:(i + 1) * CT],
                                                start=(c == 0), stop=(c == C - 1))
                last.then_inc(d_made, 1)

            def attend(i):
                pe.wait_ge(w1_out, i * B + B)
                if i > 0:
                    pe.wait_ge(x1_out, i * C)
                for c in range(C):
                    for b in range(B):
                        last = nc.tensor.matmul(bank[1 + c][:, b * CT:(b + 1) * CT],
                                                value_w[:, b, c * P:(c + 1) * P], w1[:, b, :],
                                                start=True, stop=True)
                    last.then_inc(attn_made, 1)

            def route(i):
                pe.wait_ge(x1_out, i * C + C)
                if i > 0:
                    pe.wait_ge(s_in_out, i)
                for q in range(Q):
                    for c in range(C):
                        last = nc.tensor.matmul(bank[3][:, q * E:(q + 1) * E], x1[:, c, q * P:(q + 1) * P],
                                                router[:, c, :], start=(c == 0), stop=(c == C - 1))
                last.then_inc(route_made, 1)

            def shared_units(m):
                pair = 4 + 2 * (m % 2)
                if m >= 2:
                    pe.wait_ge(shared_out, m - 1)
                for w in range(2):
                    for c in range(C):
                        last = nc.tensor.matmul(bank[pair + w][:, :].rearrange("p (b t) -> p b t", b=B),
                                                moe_sb[:, 2 * (E + 2 * m + w) + c, :], stream[:, c, :, 0:CT],
                                                start=(c == 0), stop=(c == C - 1))
                last.then_inc(up_made, 1)

            def expert_units(e):
                if e < 4:
                    pe.wait_ge(shared_out, MS - 1 if e < 2 else MS)
                else:
                    pe.wait_ge(gelu_out, e - 3)
                for c in range(C):
                    last = nc.tensor.matmul(bank[4 + e % 4][:, :].rearrange("p (b t) -> p b t", b=B),
                                            moe_sb[:, 2 * e + c, :], stream[:, c, :, 0:CT],
                                            start=(c == 0), stop=(c == C - 1))
                last.then_inc(hid_made, 1)

            pe.wait_ge(score_out, 2)
            scores(0)
            pe.wait_ge(w_in["wproj"], 16)
            pe.wait_ge(heads_made, 2 * C)
            for b in range(B):
                for m in range(C):
                    last = nc.tensor.matmul(bank[3][0:HEADS, b * D:(b + 1) * D], v_heads[:, m, b, :],
                                            wproj_sb[:, m, :], start=(m == 0), stop=(m == C - 1))
            last.then_inc(value_made, 1)
            for c in range(C):
                for m in range(C):
                    last = nc.tensor.matmul(bank[4][:, c:c + 1], wproj_sb[:, m, c * P:(c + 1) * P],
                                            no_v[:, m:m + 1], start=(m == 0), stop=(m == C - 1))
            last.then_inc(value_made, 1)
            pe.wait_ge(rep_made, 1)
            for b in range(B):
                for c in range(C):
                    last = nc.tensor.matmul(bank[5][:, b * E:(b + 1) * E], cond_rep[:, c, b, :],
                                            router_t[:, c, :], start=(c == 0), stop=(c == C - 1))
            last.then_inc(term_made, 1)
            pe.wait_ge(value_out, 2)
            attend(0)
            route(0)
            scores(1)
            pe.wait_ge(w_in["up"], 16)
            pe.wait_ge(x1_kept, 2)
            pe.wait_ge(term_out, 1)
            shared_units(0)
            attend(1)
            shared_units(1)
            route(1)
            scores(2)
            shared_units(2)
            attend(2)
            shared_units(3)
            route(2)
            scores(3)
            pe.wait_ge(s_in_out, 3)
            pe.wait_ge(w_in["wproj2"], 16)
            for m in range(C):
                for c in range(C):
                    last = nc.tensor.matmul(bank[3][:, U_COLS + m * B:U_COLS + (m + 1) * B],
                                            wproj2_sb[:, c, m * P:(m + 1) * P],
                                            cond[:, c, :], start=(c == 0), stop=(c == C - 1))
            last.then_inc(u_made, 1)
            expert_units(0)
            attend(3)
            expert_units(1)
            pe.wait_ge(w_in["wu"], 16)
            pe.wait_ge(u_out, C)
            for c in range(C):
                for m in range(C):
                    last = nc.tensor.matmul(bank[3][:, U_COLS + (C + c) * B:U_COLS + (C + c + 1) * B],
                                            wu_sb[:, m, c * P:(c + 1) * P],
                                            u_act[:, m, :], start=(m == 0), stop=(m == C - 1))
            last.then_inc(cond_made, 1)
            expert_units(2)
            expert_units(3)
            pe.wait_ge(cond_done, 1)
            expert_units(4)
            route(3)
            for e in range(5, E):
                expert_units(e)
            pe.wait_ge(w_in["down"], 16)
            pe.wait_ge(shared_out, MS)
            pe.wait_ge(gelu_out, 6)
            for c in range(C):
                for k in range(UNITS):
                    if c == 0 and k >= MS:
                        pe.wait_ge(expert_out, k - MS + 1)
                    last = nc.tensor.matmul(bank[4 + c][:, :], moe_sb[:, DOWN + c * UNITS + k, :],
                                            hidden[:, k, :], start=(k == 0), stop=(k == UNITS - 1))
                last.then_inc(moe_made, 1)

            def gate_inputs(m, first):
                for n in range(first, NXZ):
                    q, g = Q_ORDER[n // 2], n % 2
                    b = XZ_BANKS[n - first] if first else FIRST_XZ_BANKS[n]
                    if first and n == first:
                        pe.wait_ge(xz_out, m * NXZ + first)
                    if first and n == first + 1:
                        pe.wait_ge(hid, m * CT + 1)
                    for c in range(C):
                        last = nc.tensor.matmul(bank[b][:, :], x3[:, c, q * P:(q + 1) * P],
                                                wx_sb[:, c, g * XZ_COLS:(g + 1) * XZ_COLS],
                                                start=(c == 0), stop=(c == C - 1))
                    last.then_inc(xz_made, 1)

            pe.wait_ge(w_in["we"], 16)
            pe.wait_ge(w_in["wx"], 16)
            pe.wait_ge(s_in_out, CHUNKS)
            pe.wait_ge(x2_out, C)
            for c in range(C):
                for k in range(C):
                    last = nc.tensor.matmul(bank[LIN_BANKS[c]][:, :], we_sb[:, k, c * P:(c + 1) * P],
                                            x2[:, k, :], start=(k == 0), stop=(k == C - 1))
                last.then_inc(lin_made, 1)
            pe.wait_ge(x3_out, C * B)
            gate_inputs(0, 0)

            wh_v = wh_sb[:, :, :].rearrange("p c (g j m) -> p c g j m", g=4, j=J)
            staged_v = staged[:, :, :, :].rearrange("p n g (j m) -> p n g j m", j=J)
            groups = ((bank[0], GI, GF + 1, z_if, t_if), (bank[1], GC, GC + 1, z_c, t_c),
                      (bank[2], GO, GO + 1, z_o, t_o))
            pe.wait_ge(w_in["wh"], 16)
            pe.wait_ge(xz_out, 4)

            def steps(it, side=None):
                count = [pe.snap(it * U + u + 1) for u in range(U)]
                both = pe.snap(it * (16 * B) + 16 * B)
                for u in range(U):
                    now, prev, n, k = count[u], (u - 1) % U, u // HU, u % HU
                    if side:
                        side(u)
                    if k == 0:
                        pe.wait_ge(staged_in[n], both)
                    for z, g0, g1, _, taken in groups:
                        pe.wait_ge(taken, now)
                        for j in range(J):
                            last = nc.tensor.matmul(
                                z[32 * j:32 * j + B, 0:(g1 - g0) * HC].rearrange("p (g m) -> p g m", m=HC),
                                ident[:, k:k + HU + 1:HU], staged_v[:, n, g0:g1, j, :],
                                start=True, stop=False, skip_group_check=True)
                    if k == HU - 1:
                        last.then_inc(staged_used[n], 1)
                    pe.wait_ge(hid, now)
                    for z, g0, g1, made, _ in groups:
                        for c in range(C):
                            for j in range(J):
                                last = nc.tensor.matmul(
                                    z[32 * j:32 * j + B, 0:(g1 - g0) * HC].rearrange("p (g m) -> p g m", m=HC),
                                    h_ring[:, prev, c, :], wh_v[:, c, g0:g1, j, :],
                                    start=False, stop=(c == C - 1), skip_group_check=True)
                        last.then_inc(made, 1)

            def job(u, lhs, rhs, start=True, stop=True, ready=None, count=None, made=None):
                n, tile = u // Q, u % Q
                if tile == 0 and count is not None:
                    pe.wait_ge(block_in[n], count * 16 + 16)
                if u == 0:
                    ready()
                last = nc.tensor.matmul(bank[7][:, tile * P:(tile + 1) * P], lhs(n), rhs(n, tile),
                                        start=start and u == 0, stop=stop and n == 1, skip_group_check=True)
                if tile == Q - 1 and count is not None:
                    last.then_inc(block_used[n], 1)
                elif u == U - 1:
                    last.then_inc(made, 1)

            def brought(n):
                return blocks[:, n, :]

            with pe.Fori(0, CHUNKS - 1) as i:
                def tokens(n, tile):
                    return stream[:, n, tile // HALVES, bass.ds(i * CT + (CT + tile % HALVES * P), P)]

                with pe.Fori(0, E) as e:
                    steps(i * CITERS + e, lambda u: job(
                        u, brought, tokens, count=i * JOBS + e,
                        ready=lambda: pe.wait_ge(expert_taken, i * E + e + 1)))
                with pe.Fori(0, MS) as m:
                    def bank_free():
                        pe.wait_ge(expert_taken, i * E + E + 1)
                        pe.wait_ge(unit_taken, i * MS + m + 1)

                    steps(i * CITERS + m * 2 + E, lambda u: job(
                        u, brought, tokens, count=i * JOBS + m * 2 + E, ready=bank_free))
                    steps(i * CITERS + m * 2 + (E + 1), lambda u: job(
                        u, brought, tokens, count=i * JOBS + m * 2 + (E + 1),
                        ready=lambda: pe.wait_ge(gate_taken, i * MS + m + 1)))
                with pe.Fori(0, C) as c:
                    def out(r, start, stop, ready=None):
                        def units(n, tile):
                            return hidden[:, bass.ds(r * 2 + n, 1), tile * P:(tile + 1) * P
                                          ].rearrange("p a n -> p (a n)")

                        steps(i * CITERS + c * OUTS + r + UPS, lambda u: job(
                            u, brought, units, start, stop, ready or (lambda: None),
                            count=i * JOBS + c * OUTS + r + UPS))

                    def units_ready():
                        pe.wait_ge(unit_taken, i * MS + MS + 1)
                        pe.wait_ge(expert_out, i * E + 2 * E)
                        pe.wait_ge(x2_out, i * C + c + C)

                    out(0, True, False, units_ready)
                    with pe.Fori(1, OUTS - 1) as r:
                        out(r, False, False)
                    out(OUTS - 1, False, True)
                for c in range(C):
                    def x2_ready():
                        pe.wait_ge(x2_out, i * C + 2 * C)
                        if c > 0:
                            pe.wait_ge(x3_out, i * (C * B) + (C * B + c * B))

                    steps(i * CITERS + JOBS + c, lambda u: job(
                        u, lambda n: we_sb[:, n, c * P:(c + 1) * P],
                        lambda n, tile: x2[:, n, tile * P:(tile + 1) * P], ready=x2_ready, made=lin_made))
                with pe.Fori(0, SIDE_XZ) as g:
                    def x3_ready():
                        pe.wait_ge(x3_out, i * (C * B) + 2 * C * B)
                        pe.wait_ge(xz_out, i * NXZ + g + NXZ)

                    steps(i * CITERS + g + (JOBS + C), lambda u: job(
                        u, lambda n: x3[:, n, Q_ORDER[0] * P:(Q_ORDER[0] + 1) * P],
                        lambda n, tile: wx_sb[:, n, bass.ds(g * XZ_COLS + tile * P, P)],
                        ready=x3_ready, made=xz_made))
                gate_inputs(i + 1, SIDE_XZ)
                pe.wait_ge(xz_out, i * NXZ + (2 * NXZ - 2))
            with pe.Fori(0, CITERS) as k:
                steps(k + (CHUNKS - 1) * CITERS)


_INS = ("x", "small", "wkv", "wq", "wproj", "moe", "wu", "we", "wproj2", "wx",
        "wh", "bias_z")


def kernel(**inputs):
    import numpy as np
    import concourse.bacc as bacc
    from concourse.bass_utils import run_bass_kernel_spmd

    a = {k: np.asarray(v) for k, v in inputs.items()}

    def fold_rows(w):
        n = w.shape[1]
        return w.reshape(4, 2, 32, n).transpose(0, 2, 1, 3).reshape(P, C, n)

    def fold_cols(w):
        n = w.shape[0]
        return w.reshape(n, 4, 2, 32).transpose(0, 2, 1, 3).reshape(n, D)

    def plain_rows(w):
        return w.reshape(-1, P, w.shape[1]).transpose(1, 0, 2)

    def vector(v):
        return plain_rows(v.reshape(-1, 1))[:, :, 0]

    f = np.float32
    heads = (np.arange(D)[:, None] // (D // HEADS) == np.arange(HEADS)[None, :]).astype(f)
    before = (np.arange(E)[None, :] < np.arange(E)[:, None]).astype(f).reshape(1, E * E)
    parts = {
        "cond": fold_rows(a["cond_1024"].T),
        "b_q": vector(a["L0_cond_b_q"]),
        "b_kv": vector(a["L0_cond_b_kv"]),
        "no_k": vector(a["L0_cond_no_op_k"].reshape(-1)),
        "no_v": vector(a["L0_cond_no_op_v"].reshape(-1)),
        "b_proj": fold_rows(a["L0_cond_b_proj"].reshape(D, 1)),
        "b_proj2": vector(a["L2_cond_b_proj"]),
        "router": fold_rows(a["L1_cond_router_w"].T),
        "router_t": fold_rows(a["L1_cond_router_t_w"].T),
        "router_bias": np.broadcast_to(a["L1_cond_router_bias"][None, :], (P, E)),
        "head": plain_rows(heads),
        "before": np.broadcast_to(before, (P, E * E)),
        "ident": np.eye(P, 16, dtype=f),
    }
    ups = []
    for e in range(E):
        ups.append(fold_rows(a["L1_cond_rw1"].reshape(E, P, D)[e].T))
    for m in range(MS):
        for name in ("L1_cond_sw1", "L1_cond_sw3"):
            ups.append(fold_rows(a[name][m * P:(m + 1) * P].T))
    down = [plain_rows(fold_cols(a["L1_cond_sw2"].T))]
    down += [fold_cols(w.T)[:, None, :] for w in a["L1_cond_rw2"]]
    down = np.concatenate(down, axis=1)
    downs = [down[:, :, c * P:(c + 1) * P] for c in range(C)]
    arrays = {
        "x": a["x"].reshape(B, T, 4, 2, 32).transpose(2, 4, 3, 0, 1).reshape(P, C, B, T),
        "small": np.concatenate([parts[n].reshape(P, -1) for n in SMALL], axis=1),
        "wkv": fold_rows(a["L0_cond_W_kv"]),
        "wq": plain_rows(fold_cols(a["L0_cond_W_q"].T)),
        "wproj": plain_rows(fold_cols(a["L0_cond_W_proj"])),
        "moe": np.concatenate(ups + downs, axis=1),
        "wu": plain_rows(fold_cols(a["L2_cond_weight_matrix"][:D])),
        "we": fold_rows(fold_cols(a["L2_cond_weight_matrix"][D:])),
        "wproj2": fold_rows(a["L2_cond_W_proj"]),
        "wx": fold_rows(a["L3_cond_Wx"]),
        "wh": fold_rows(a["L3_cond_Wh"]),
        "bias_z": np.broadcast_to(a["L3_cond_b"][None, :], (P, G4)),
    }
    nc = bacc.Bacc("TRN2", target_bir_lowering=False, num_devices=1)
    feed, args = {}, []
    for name in _INS:
        v = np.ascontiguousarray(arrays[name])
        feed[f"in_{name}"] = v
        args.append(nc.dram_tensor(f"in_{name}", v.shape, mybir.dt.from_np(v.dtype), kind="ExternalInput").ap())
    args.append(nc.dram_tensor("out_y", (P, C, B, T), F32, kind="ExternalOutput").ap())
    cond_stack_kernel(nc, *args)
    r = run_bass_kernel_spmd(nc, [feed], core_ids=[0])
    y = r.results[0]["out_y"]
    return np.ascontiguousarray(
        y.reshape(4, 32, C, B, T).transpose(3, 4, 0, 2, 1).reshape(B, T, D))
```
